# Optimizing a Trainium2 kernel written in Bass

```python
import numpy as np
import jax
import jax.numpy as jnp

def _softmax(x, axis=-1):
    return jax.nn.softmax(x, axis=axis)

def _gelu(x):
    return jax.nn.gelu(x, approximate=True)

def _silu(x):
    return jax.nn.silu(x)

def _sigmoid(x):
    return jax.nn.sigmoid(x)

def _layernorm(x, axis=-1, eps=1e-05):
    m = jnp.mean(x, axis=axis, keepdims=True)
    v = jnp.var(x, axis=axis, keepdims=True)
    return (x - m) / jnp.sqrt(v + eps)

def _scatter_add(tgt, idx, src, axis=0):
    return tgt.at[idx].add(src)

def _segment_sum(src, seg, n):
    return jax.ops.segment_sum(src, seg, n)
kernel_name = 'mk_adj_resnorm_d1_adj_r2_5afd79'

def setup_inputs(seed: int=0):
    np.random.seed(seed)
    _w = jnp.asarray

    def _rec_inputs():
        import jax
        import jax.numpy as jnp
        _gk = jax.random.key(seed)
        x = -0.0005146 + 1 * jax.random.normal(jax.random.fold_in(_gk, 1), (8, 1024, 128), jnp.float32)
        _w = (1.0 + jnp.arange(1024, dtype=jnp.float32)) ** (-0.5)
        _w = _w / _w.mean()
        _pij = jnp.clip(0.0078125 * _w[:, None] * _w[None, :], 0.0, 1.0)
        _a = jax.random.uniform(jax.random.fold_in(_gk, 2), (8, 1024, 1024)) < _pij
        adj = _a.astype(jnp.int32)
        return (x, adj)
    x, adj = _rec_inputs()

    def _L0_gnn_setup():
        import jax, jax.numpy as jnp
        import numpy as np
        B, N, C, OUT, S = (4, 1024, 128, 128, 25)
        DENSITY = 0.008
        key = jax.random.key(seed)
        kA, kX, kW = jax.random.split(key, 3)
        A = jax.random.bernoulli(kA, DENSITY, (B, N, N)).astype(jnp.int32)
        X = jax.random.normal(kX, (B, N, C), dtype=jnp.float32)
        W = jax.random.normal(kW, (2 * C, OUT), dtype=jnp.float32) * np.float32(1.0 / np.sqrt(2 * C))
        b = jnp.zeros((OUT,), dtype=jnp.float32)
        return {'A': A, 'X': X, 'W': W, 'b': b}
    _L0_gnn_all = _L0_gnn_setup()
    _L0_gnn_in = {k: v for k, v in _L0_gnn_all.items() if k in ('W', 'b')}
    del _L0_gnn_all
    return {'x': x, 'adj': adj, 'L0_gnn_W': _L0_gnn_in['W'], 'L0_gnn_b': _L0_gnn_in['b']}

def reference(x, adj, L0_gnn_W, L0_gnn_b):
    import jax
    import jax.numpy as jnp

    def _L0_gnn_ref(A, X, W, b):
        import jax, jax.numpy as jnp
        import numpy as np
        B, N, C, OUT, S = (4, 1024, 128, 128, 25)
        DENSITY = 0.008
        mask = A != 0
        neg_inf = jnp.float32(-jnp.inf)
        pri = -jnp.arange(N, dtype=jnp.float32)
        scores = jnp.where(mask, pri, neg_inf)
        vals, idx = jax.lax.top_k(scores, S)
        valid = vals > neg_inf
        feats = jax.vmap(lambda x, i: x[i])(X, idx)
        feats = jnp.where(valid[..., None], feats, neg_inf)
        agg = feats.max(axis=2)
        degree = mask.sum(axis=-1)
        agg = jnp.where((degree <= S)[..., None], jnp.maximum(agg, 0.0), agg)
        h = jnp.concatenate([X, agg], axis=-1)
        out = jax.nn.relu(jnp.einsum('bnf,fo->bno', h, W) + b)
        return out
    x = _layernorm(x + _L0_gnn_ref(adj, x, L0_gnn_W, L0_gnn_b), axis=-1)
    return x

_drawn_inputs = setup_inputs


def setup_inputs(seed=0):
    import zlib

    import numpy as np

    out = dict(_drawn_inputs(seed))
    spreads = {'L0_gnn_b': (0.0, 0.1)}
    factors = {}
    for name, (base, spread) in spreads.items():
        noise = np.random.default_rng([zlib.crc32(name.encode()), seed]).standard_normal(out[name].shape)
        drawn = base * np.exp(spread * noise) if base else spread * noise
        out[name] = jnp.asarray(drawn.astype(out[name].dtype))
    for name, factor in factors.items():
        out[name] = (out[name] * factor).astype(out[name].dtype)
    return out
```

```python
import concourse.bass as bass
from concourse import mybir
from contextlib import ExitStack
F32=mybir.dt.float32; BF16=mybir.dt.bfloat16; I32=mybir.dt.int32; U32=mybir.dt.uint32
ALU=mybir.AluOpType; ACT=mybir.ActivationFunctionType; AX=mybir.AxisListType
P=128
def build(nc, x, adj, W, b, out):
    B,N,C=x.shape
    K=25
    TPB=N//P; T=B*TPB
    BIG=3.0e38
    xr=x.rearrange("b n c -> (b n) c"); outr=out.rearrange("b n c -> (b n) c")
    xt=x.rearrange("b (t p) c -> (b t) p c",p=P)
    ot=out.rearrange("b (t p) c -> (b t) p c",p=P)
    at=adj.rearrange("b (t p) n -> (b t) p n",p=P)
    ctx=ExitStack()
    with ctx:
        sb=lambda n,s,d: ctx.enter_context(nc.sbuf_tensor(n,s,d))
        ps=lambda n,s,d: ctx.enter_context(nc.psum_tensor(n,s,d))
        sem=lambda n: ctx.enter_context(nc.semaphore(n))
        adj_sb=sb("adj_sb",[P,2,N],I32)
        xs=sb("xs",[P,2,C],F32)
        w_sb=sb("w_sb",[P,2,C],F32)
        bias=sb("bias",[1,C],F32)
        ones=sb("ones",[1,P],F32)
        desc=sb("desc",[P,N],F32)
        base=sb("base",[P,T],F32)
        score=sb("score",[P,N],F32)
        val=sb("val",[P,32],F32)
        fill=sb("fill",[P,K],F32)
        idx=sb("idx",[P,2,K],I32)
        z=sb("z",[P,2,2],F32)
        g=sb("g",[P,2,K,C],F32)
        agg=sb("agg",[P,C],F32)
        aggm=sb("aggm",[P,C],F32)
        ident=sb("ident",[P,P],F32)
        tT=sb("tT",[P,2,P],F32)
        y=sb("y",[P,C],F32)
        st=sb("st",[P,6],F32); mv=sb("mv",[P,2],F32); sd=sb("sd",[P,1],F32); rs=sb("rs",[P,1],F32)
        o=sb("o",[P,2,C],F32)
        eps=sb("eps",[P,1],F32)
        pT=ps("pT",[P,2,P],F32); pO=ps("pO",[P,C],F32)
        s_const=sem("const_loaded"); s_iota=sem("tables_ready")
        s_adj=[sem(f"adj_loaded{u}") for u in range(2)]; s_x=[sem(f"x_loaded{u}") for u in range(2)]; s_xfree=sem("x_used")
        s_adjfree=sem("adj_used"); s_idx=sem("idx_ready"); s_g=[sem(f"gathered{u}") for u in range(2)]
        s_gfree=sem("gather_used"); s_agg=sem("agg_ready"); s_tp=sem("transposed"); s_tc=sem("transposes_copied")
        s_mm=sem("out_product"); s_y=sem("y_ready"); s_var=sem("var_ready"); s_sd=sem("std_ready"); s_o=sem("o_ready")
        s_st=[sem(f"stored{u}") for u in range(2)]
        s_ch=sem("chain")
        block=ctx.enter_context(nc.Block())
        @block.sync
        def _(sp):
            sp.dma_start(w_sb[:,:,:],W.rearrange("(h f) o -> f h o",h=2)).then_inc(s_const,16)
            sp.dma_start(bias[:,:],b.rearrange("(a d) -> a d",a=1)).then_inc(s_const,16)
            with sp.Fori(0,T//2) as i:
                for u in range(2):
                    sp.wait_ge(s_adjfree,2*i+u+1)
                    sp.dma_start(adj_sb[:,u,:],at[bass.ds(2*i+u,1),:,:].rearrange("a p n -> p (a n)")).then_inc(s_adj[u],16)
                    sp.wait_ge(s_xfree,2*i+u+1)
                    sp.dma_start(xs[:,u,:],xt[bass.ds(2*i+u,1),:,:].rearrange("a p n -> p (a n)")).then_inc(s_x[u],16)
        @block.gpsimd
        def _(pool):
            pool.iota(desc[:,:],[[-1,N]],base=N,channel_multiplier=0,allow_small_or_imprecise_dtypes=True).then_inc(s_iota,1)
            pool.iota(base[:,:],[[N,B],[0,TPB]],base=N,channel_multiplier=0,allow_small_or_imprecise_dtypes=True).then_inc(s_iota,1)
            pool.memset(ident[:,:],0.0).then_inc(s_ch,1)
            pool.wait_ge(s_ch,1)
            pool.affine_select(out=ident[:,:],in_=ident[:,:],compare_op=ALU.not_equal,fill=1.0,base=0,pattern=[[-1,P]],channel_multiplier=1).then_inc(s_iota,1)
            pool.memset(ones[:,:],1.0).then_inc(s_iota,1)
            pool.memset(eps[:,:],1e-5).then_inc(s_iota,1)
            with pool.Fori(0,T//2) as i:
                for u in range(2):
                    pool.wait_ge(s_idx,2*i+u+1)
                    pool.wait_ge(s_gfree,2*i+u+1)
                    pool.nop(nofuse=True)
                    for k in range(K):
                        pool.indirect_dma_start(out=g[:,u,k,:],out_offset=None,in_=xr,in_offset=bass.IndirectOffsetOnAxis(ap=idx[:,u,k:k+1],axis=0)).then_inc(s_g[u],16)
        @block.vector
        def _(v):
            v.sem_inc(s_adjfree,2); v.sem_inc(s_gfree,2); v.sem_inc(s_xfree,2)
            v.wait_ge(s_iota,5)
            def extract(i,u,t):
                v.wait_ge(s_adj[u],16*(i+1))
                v.scalar_tensor_tensor(out=score[:,:],in0=adj_sb[:,u,:],scalar=0.0,in1=desc[:,:],op0=ALU.not_equal,op1=ALU.mult).then_inc(s_adjfree,1)
                v.drain()
                for r in range(4):
                    v.max(val[:,8*r:8*r+8],score[:,:]); v.drain()
                    if r<3:
                        v.match_replace(score[:,:],val[:,8*r:8*r+8],score[:,:],0.0); v.drain()
                v.scalar_tensor_tensor(out=fill[:,:],in0=val[:,0:K],scalar=0.0,in1=val[:,0:1].to_broadcast([P,K]),op0=ALU.is_equal,op1=ALU.mult); v.drain()
                v.tensor_tensor(fill[:,:],fill[:,:],val[:,0:K],ALU.max); v.drain()
                v.tensor_scalar(fill[:,:],fill[:,:],1.0,None,ALU.max); v.drain()
                v.tensor_scalar(z[:,u,0:1],val[:,K:K+1],0.0,-BIG,ALU.is_gt,ALU.mult)
                v.tensor_scalar(z[:,u,1:2],val[:,0:1],0.0,None,ALU.is_gt)
                v.scalar_tensor_tensor(out=idx[:,u,:],in0=fill[:,:],scalar=-1.0,in1=base[:,bass.ds(t,1)].to_broadcast([P,K]),op0=ALU.mult,op1=ALU.add).then_inc(s_idx,1)
                v.drain()
            def finish(i,u,t):
                v.wait_ge(s_g[u],16*K*(i+1))
                v.tensor_reduce(agg[:,:],g[:,u,:,:].rearrange("p k f -> p f k"),AX.X,ALU.max).then_inc(s_gfree,1)
                v.drain()
                v.tensor_scalar(aggm[:,:],agg[:,:],z[:,u,0:1],z[:,u,1:2],ALU.max,ALU.mult).then_inc(s_agg,1)
                v.wait_ge(s_tp,t+1)
                v.tensor_copy(tT[:,:,:],pT[:,:,:]).then_inc(s_tc,1)
                v.wait_ge(s_mm,t+1)
                v.wait_ge(s_x[u],16*(i+1))
                v.scalar_tensor_tensor(out=y[:,:],in0=pO[:,:],scalar=0.0,in1=xs[:,u,:],op0=ALU.max,op1=ALU.add).then_inc(s_xfree,1); v.drain()
                v.bn_stats(st[:,:],y[:,:]); v.drain()
                v.bn_aggr(mv[:,:],st[:,:]).then_inc(s_var,1)
                v.wait_ge(s_sd,t+1)
                v.reciprocal(rs[:,:],sd[:,:]); v.drain()
                v.wait_ge(s_st[u],16*(i+1))
                v.tensor_scalar(o[:,u,:],y[:,:],mv[:,0:1],rs[:,0:1],ALU.subtract,ALU.mult).then_inc(s_o,1)
            extract(0,0,0)
            with v.Fori(0,T//2-1) as i:
                extract(i,1,2*i+1)
                finish(i,0,2*i)
                extract(i+1,0,2*i+2)
                finish(i,1,2*i+1)
            i=T//2-1
            extract(i,1,2*i+1)
            finish(i,0,2*i)
            finish(i,1,2*i+1)
        @block.tensor
        def _(pe):
            pe.wait_ge(s_iota,5); pe.wait_ge(s_const,32)
            with pe.Fori(0,T//2) as i:
                for u in range(2):
                    t=2*i+u
                    pe.wait_ge(s_x[u],16*(i+1))
                    pe.wait_ge(s_tc,t+1)
                    pe.transpose(pT[:,0,:],xs[:,u,:],ident[:,:])
                    pe.wait_ge(s_agg,t+1)
                    pe.transpose(pT[:,1,:],aggm[:,:],ident[:,:]).then_inc(s_tp,1)
                    pe.wait_ge(s_tc,t+2)
                    pe.matmul(pO[:,:],tT[:,0,:],w_sb[:,0,:],start=True,stop=False)
                    pe.matmul(pO[:,:],tT[:,1,:],w_sb[:,1,:],start=False,stop=False)
                    pe.matmul(pO[:,:],ones[:,:],bias[:,:],start=False,stop=True).then_inc(s_mm,1)
        @block.scalar
        def _(a):
            a.sem_inc(s_tc,1); a.sem_inc(s_st[0],16); a.sem_inc(s_st[1],16)
            a.wait_ge(s_iota,5)
            with a.Fori(0,T//2) as i:
                for u in range(2):
                    t=2*i+u
                    a.wait_ge(s_var,t+1)
                    a.activation(sd[:,:],mv[:,1:2],ACT.Sqrt,bias=eps[:,0:1]).then_inc(s_sd,1)
                    a.wait_ge(s_o,t+1)
                    a.dma_start(ot[bass.ds(t,1),:,:].rearrange("a p n -> p (a n)"),o[:,u,:]).then_inc(s_st[u],16)
            for u in range(2):
                a.wait_ge(s_st[u],16*(T//2+1))

def kernel(x, adj, L0_gnn_W, L0_gnn_b):
    import numpy as np
    import concourse.bacc as bacc
    from concourse.bass_utils import run_bass_kernel_spmd as run
    nc=bacc.Bacc("TRN2",target_bir_lowering=False,num_devices=1)
    arrays={}; args=[]
    for name,a in (("x",x),("adj",adj),("W",L0_gnn_W),("b",L0_gnn_b)):
        a=np.ascontiguousarray(a)
        arrays["in_"+name]=a
        args.append(nc.dram_tensor("in_"+name,a.shape,mybir.dt.from_np(a.dtype),kind="ExternalInput").ap())
    o=nc.dram_tensor("out",x.shape,F32,kind="ExternalOutput").ap()
    build(nc,*args,o)
    r=run(nc,[arrays],core_ids=[0])
    return r.results[0]["out"]
```

```python
import concourse.bass as bass
from concourse import mybir
from contextlib import ExitStack

F32 = mybir.dt.float32
BF16 = mybir.dt.bfloat16
I32 = mybir.dt.int32
ALU = mybir.AluOpType
ACT = mybir.ActivationFunctionType
AX = mybir.AxisListType

P = 128
K = 25
EPS = 1e-5
BIG = 3.0e38
MARK = 256
RANKS8 = 8
ROUNDS = -(-(K + 1) // RANKS8)


def build(nc, x, adj, W, b, out):
    B, N, C = x.shape
    NT = N // P
    MT = NT - 1
    MAIN = B * MT
    STATIC = 5
    EXTRA = 2
    DEPTH = [(8, 4), (10, 6), (12, 8)]
    LEVELS = len(DEPTH)

    x_rows = x.rearrange("b n c -> (b n) c")
    x_tiles = x.rearrange("b (t p) c -> b p t c", p=P)
    out_tiles = out.rearrange("b (t p) c -> b p t c", p=P)
    adj_tiles = adj.rearrange("b (t p) n -> (b t) p n", p=P)

    ctx = ExitStack()
    with ctx:
        def sb(name, shape, dt):
            return ctx.enter_context(nc.sbuf_tensor(name, shape, dt))

        def psum(name, shape, dt):
            return ctx.enter_context(nc.psum_tensor(name, shape, dt))

        def sem(name):
            return ctx.enter_context(nc.semaphore(name))

        w_sb = sb("w_sb", [P, 2, C], F32)
        bias = sb("bias", [1, C], F32)
        ones_row = sb("ones_row", [1, P], F32)
        ones_bf = sb("ones_bf", [P, 1], BF16)
        eps = sb("eps", [P, 1], F32)
        falling = sb("falling", [P, N], F32)
        row_base = sb("row_base", [P, B], F32)
        iota_work = sb("iota_work", [P, P], F32)
        ident = sb("ident", [P, P], F32)
        ident_bf = sb("ident_bf", [P, P], BF16)
        rank_of = sb("rank_of", [P, P], F32)
        rank_bf = sb("rank_bf", [P, P], BF16)
        depth_tab = sb("depth_tab", [P, LEVELS, MT, NT], F32)
        x_sb = sb("x_sb", [P, 2, NT, C], F32)
        x_part = sb("x_part", [P, 2, 3, NT, C], BF16)
        x_rest = sb("x_rest", [P, 2, NT, C], F32)
        adj_sb = sb("adj_sb", [P, 2, N], I32)
        mask = sb("mask", [P, 2, N], BF16)
        maskT = sb("maskT", [P, 2, N], BF16)
        V = sb("V", [P, 2, MT, NT, P], BF16)
        hot0 = sb("hot0", [P, 2, DEPTH[0][0], P], BF16)
        hot = sb("hot", [P, 2, MT, DEPTH[0][1], P], BF16)
        hotx = sb("hotx", [P, 2, NT, 2, P], BF16)
        viol = sb("viol", [P, LEVELS * MT * NT + MT], BF16)
        degree = sb("degree", [P, MT], F32)
        vsum = sb("vsum", [1, LEVELS * MT], F32)
        vdeg = sb("vdeg", [1, MT], F32)
        vlow = sb("vlow", [1, MT], F32)
        vhigh = sb("vhigh", [1, MT], F32)
        level = sb("level", [1, 2, MT], I32)
        part = sb("part", [P, 2, STATIC, P], F32)
        more = sb("more", [P, P], F32)
        agg_t = sb("agg_t", [P, 2, P], F32)
        xt_sb = sb("xt_sb", [P, 2, P], F32)
        g_adj = [sb(f"g_adj{w}", [P, N], I32) for w in range(2)]
        g_score = [sb(f"g_score{w}", [P, N], F32) for w in range(2)]
        g_val = [sb(f"g_val{w}", [P, RANKS8 * ROUNDS], F32) for w in range(2)]
        g_pick = [sb(f"g_pick{w}", [P, K], F32) for w in range(2)]
        g_bound = [sb(f"g_bound{w}", [P, 2, 2], F32) for w in range(2)]
        g_idx = [sb(f"g_idx{w}", [P, K], I32) for w in range(2)]
        g_feat = [sb(f"g_feat{w}", [P, K, C], F32) for w in range(2)]
        g_max = [sb(f"g_max{w}", [P, C], F32) for w in range(2)]
        g_agg = [sb(f"g_agg{w}", [P, C], F32) for w in range(2)]
        agg0_t = sb("agg0_t", [P, P], F32)
        x0_t = sb("x0_t", [P, P], F32)
        y_sb = sb("y_sb", [P, 2, NT, C], F32)
        stats = sb("stats", [P, 2, NT, 6], F32)
        mv = sb("mv", [P, 2, NT, 2], F32)
        std = sb("std", [P, 2, NT], F32)
        rstd = sb("rstd", [P, 2, NT], F32)

        pairs = [psum(f"pair{i}", [P, 2, 4, P], F32) for i in range(2)]
        half = psum("half", [P, 4, P], F32)
        p_maskT = psum("p_maskT", [P, N], BF16)
        p_V = psum("p_V", [P, N // 2], F32)
        misc = psum("misc", [P, 512], F32)
        p_out = misc[:, 0:C]
        p_xt = p_V[:, 0:P]
        p_cnt = misc[:, P:P + MT * NT]
        NV = LEVELS * MT * NT + MT
        p_viol = misc[0:1, 2 * P:2 * P + NV]

        s_const = sem("weights_loaded")
        s_tab = sem("tables_ready")
        s_ptab = sem("pool_table_step")
        s_tab2 = sem("bf16_tables_ready")
        s_x = [sem(f"x_loaded{q}") for q in range(2)]
        s_split = sem("x_split_ready")
        s_splitstep = sem("x_split_step")
        s_adj = [sem(f"adj_loaded{u}") for u in range(2)]
        s_mask = sem("mask_ready")
        s_mT = sem("mask_transposed")
        s_mTc = sem("maskT_ready")
        s_Vp = sem("V_product")
        s_V = sem("V_ready")
        s_cnt = sem("counts_ready")
        s_viol = sem("violations_ready")
        s_vp = sem("violations_summed")
        s_level = sem("level_ready")
        s_hot = sem("onehots_ready")
        s_pair = sem("picked")
        s_used = sem("picked_reduced")
        s_hotx = sem("extra_onehots_ready")
        s_xpair = sem("extra_picked")
        s_xused = sem("extra_reduced")
        s_agg = sem("agg_ready")
        s_xt = sem("x_transposed")
        s_xtc = sem("xT_ready")
        s_out = sem("linear_done")
        s_y = sem("residual_added")
        s_var = sem("variance_ready")
        s_std = sem("std_ready")
        s_norm = sem("normalised")
        s_store = [sem(f"stored{q}") for q in range(2)]
        s_adj0 = sem("adj0_loaded")
        s_score0 = sem("adj0_used")
        s_idx0 = sem("idx0_ready")
        s_g0 = sem("gathered0")
        s_g0max = sem("gathered0_reduced")
        s_agg0 = sem("agg0_ready")
        s_agg0t = sem("agg0_transposed")
        s_agg0c = sem("agg0T_ready")
        s_x0t = sem("x0_transposed")
        s_x0c = sem("x0T_ready")
        s_out0 = sem("linear0_done")
        s_fstep = sem("redo_step")
        s_fdma = sem("redo_dma")
        s_fadj = sem("redo_adj_ready")
        s_fidx = sem("redo_idx_ready")
        s_fg = sem("redo_gathered")
        s_fagg = sem("redo_agg_ready")
        s_ft = sem("redo_transposed")

        def pos(i, q, s):
            return 2 * MT * i + MT * q + (s - 1)

        def par(q, s):
            return (MT * q + s - 1) % 2

        def nth(i, q, s):
            return MT * i + (MT * q + s - 1) // 2 + 1

        ORDER = {1: 0, 2: 1, 3: 2, 4: 3, 5: 4, 0: 5, 6: 6, 7: 7}

        def batches(eng, prologue, step):
            prologue()
            with eng.Fori(0, B // 2 - 1) as i:
                step(i, 0, False)
                step(i, 1, False)
            step(B // 2 - 1, 0, False)
            step(B // 2 - 1, 1, True)

        block = ctx.enter_context(nc.Block())

        @block.sync
        def _(sp):
            def load_x(i, q):
                sp.dma_start(x_sb[:, q], x_tiles[bass.ds(2 * i + q, 1)].rearrange("a p t c -> p (a t) c")
                             ).then_inc(s_x[q], 16)

            def load_adj(i, q, s):
                sp.dma_start(adj_sb[:, par(q, s)], adj_tiles[bass.ds(2 * NT * i + NT * q + s, 1)]
                             .rearrange("a p n -> p (a n)")).then_inc(s_adj[par(q, s)], 16)

            def load_adj0(i, q):
                sp.dma_start(g_adj[0][:, :], adj_tiles[bass.ds(2 * NT * i + NT * q, 1)]
                             .rearrange("a p n -> p (a n)")).then_inc(s_adj0, 16)

            def prologue():
                load_adj(0, 0, 1)
                load_adj(0, 0, 2)
                load_x(0, 0)
                load_adj0(0, 0)
                sp.dma_start(w_sb[:, :, :], W.rearrange("(h f) o -> f h o", h=2)).then_inc(s_const, 16)
                sp.dma_start(bias[:, :], b.rearrange("(a d) -> a d", a=1)).then_inc(s_const, 16)
                for s in range(3, NT):
                    sp.wait_ge(s_mask, s - 2)
                    load_adj(0, 0, s)

            def step(i, q, last):
                ni, nq = (i, 1) if q == 0 else (i + 1, 0)
                first = isinstance(i, int) and i == 0 and q == 0
                if not last:
                    for s in range(1, NT):
                        sp.wait_ge(s_mask, pos(ni, nq, s) - 1)
                        load_adj(ni, nq, s)
                        if s == 1:
                            sp.wait_ge(s_score0, 2 * i + q + 1)
                            load_adj0(ni, nq)
                        if s == 2:
                            sp.wait_ge(s_y, NT * (2 * i + q))
                            load_x(ni, nq)
                        if s == 5:
                            store(i, q, first)
                else:
                    store(i, q, False)

            def store(i, q, first):
                pi, pq = (i, 0) if q == 1 else (i - 1, 1)
                sp.wait_ge(s_norm, 2 * i + q)
                sp.dma_start(out_tiles[bass.ds(2 * pi + pq, 1)].rearrange("a p t c -> p (a t) c"),
                             y_sb[:, pq]).then_inc(s_store[pq], 16)

            prologue()
            def step_first():
                for s in range(1, NT):
                    sp.wait_ge(s_mask, pos(0, 1, s) - 1)
                    load_adj(0, 1, s)
                    if s == 1:
                        sp.wait_ge(s_score0, 1)
                        load_adj0(0, 1)
                        load_x(0, 1)
            step_first()
            step(0, 1, False)
            with sp.Fori(1, B // 2 - 1) as i:
                step(i, 0, False)
                step(i, 1, False)
            step(B // 2 - 1, 0, False)
            step(B // 2 - 1, 1, True)
            sp.wait_ge(s_norm, B)
            sp.dma_start(out_tiles[B - 1], y_sb[:, 1]).then_inc(s_store[1], 16)
            sp.wait_ge(s_store[0], 16 * (B // 2))
            sp.wait_ge(s_store[1], 16 * (B // 2))

        @block.gpsimd
        def _(pool):
            pool.memset(ident[:, :], 0.0).then_inc(s_ptab, 1)
            pool.memset(iota_work[:, :], 1.0).then_inc(s_ptab, 1)
            pool.memset(ones_row[:, :], 1.0).then_inc(s_tab, 1)
            pool.memset(ones_bf[:, :], 1.0).then_inc(s_tab, 1)
            pool.memset(eps[:, :], EPS).then_inc(s_tab, 1)
            pool.wait_ge(s_ptab, 2)
            pool.affine_select(out=ident[:, :], in_=ident[:, :], compare_op=ALU.not_equal, fill=1.0,
                               base=0, pattern=[[-1, P]], channel_multiplier=1).then_inc(s_ptab, 1)
            pool.affine_select(out=iota_work[:, :], in_=iota_work[:, :], compare_op=ALU.is_ge, fill=0.0,
                               base=0, pattern=[[1, P]], channel_multiplier=-1).then_inc(s_ptab, 1)
            pool.wait_ge(s_ptab, 4)
            pool.affine_select(out=rank_of[:, :], in_=iota_work[:, :], compare_op=ALU.not_equal,
                               fill=1.0 - MARK, base=0, pattern=[[-1, P]],
                               channel_multiplier=1).then_inc(s_tab, 1)
            pool.iota(falling[:, :], [[-1, N]], base=N, channel_multiplier=0,
                      allow_small_or_imprecise_dtypes=True).then_inc(s_tab, 1)
            pool.iota(row_base[:, :], [[N, B]], base=N, channel_multiplier=0,
                      allow_small_or_imprecise_dtypes=True).then_inc(s_tab, 1)
            for lv, (d0, d) in enumerate(DEPTH):
                pool.memset(depth_tab[:, lv, :, 0:1], float(d0)).then_inc(s_tab, 1)
                pool.memset(depth_tab[:, lv, :, 1:NT], float(d)).then_inc(s_tab, 1)

            def split(i, q):
                n = 4 * (2 * i + q)
                pool.wait_ge(s_x[q], 16 * (i + 1))
                pool.nop(nofuse=True)
                pool.tensor_copy(x_part[:, q, 0], x_sb[:, q]).then_inc(s_splitstep, 1)
                pool.wait_ge(s_splitstep, n + 1)
                pool.nop(nofuse=True)
                pool.tensor_tensor(x_rest[:, 0], x_sb[:, q], x_part[:, q, 0], ALU.subtract).then_inc(s_splitstep, 1)
                pool.wait_ge(s_splitstep, n + 2)
                pool.nop(nofuse=True)
                pool.tensor_copy(x_part[:, q, 1], x_rest[:, 0]).then_inc(s_splitstep, 1)
                pool.wait_ge(s_splitstep, n + 3)
                pool.nop(nofuse=True)
                pool.tensor_tensor(x_rest[:, 1], x_rest[:, 0], x_part[:, q, 1], ALU.subtract).then_inc(s_splitstep, 1)
                pool.wait_ge(s_splitstep, n + 4)
                pool.nop(nofuse=True)
                pool.tensor_copy(x_part[:, q, 2], x_rest[:, 1]).then_inc(s_split, 1)

            def gather(w, signal):
                for k in range(K):
                    pool.indirect_dma_start(
                        out=g_feat[w][:, k, :], out_offset=None, in_=x_rows,
                        in_offset=bass.IndirectOffsetOnAxis(ap=g_idx[w][:, k:k + 1], axis=0)).then_inc(signal, 16)

            def gather0(i, q):
                pool.wait_ge(s_idx0, 2 * i + q + 1)
                if not (isinstance(i, int) and i == 0 and q == 0):
                    pool.wait_ge(s_g0max, 2 * i + q)
                pool.nop(nofuse=True)
                gather(0, s_g0)

            def redo(i, q, s):
                m = pos(i, q, s)
                if s == 1:
                    pool.wait_ge(s_level, 2 * i + q + 1)
                    pool.nop(nofuse=True)
                lv = pool.value_load(level[0:1, q, s - 1:s], min_val=0, max_val=LEVELS)
                with pool.If(lv == LEVELS):
                    pool.dma_start(g_adj[1][:, :], adj_tiles[bass.ds(2 * NT * i + NT * q + s, 1)]
                                   .rearrange("a p n -> p (a n)")).then_inc(s_fdma, 16)
                    pool.wait_ge(s_fdma, 16)
                    pool.sem_inc(s_fadj, 1)
                    pool.wait_ge(s_fidx, m + 1)
                    pool.nop(nofuse=True)
                    gather(1, s_fdma)
                    pool.wait_ge(s_fdma, 16 * (K + 1))
                    pool.sem_clear(s_fdma)
                    pool.sem_inc(s_fg, 1)
                with pool.Else():
                    pool.sem_inc(s_fadj, 1)
                    pool.sem_inc(s_fg, 1)

            def prologue():
                split(0, 0)
                gather0(0, 0)

            def step(i, q, last):
                ni, nq = (i, 1) if q == 0 else (i + 1, 0)
                for s in range(1, 5):
                    redo(i, q, s)
                    if s == 3 and not last:
                        split(ni, nq)
                if not last:
                    gather0(ni, nq)
                for s in range(5, NT):
                    redo(i, q, s)

            batches(pool, prologue, step)

        @block.scalar
        def _(act):
            act.wait_ge(s_tab, 6 + 2 * LEVELS)
            nc.scalar.activation(ident_bf[:, :], ident[:, :], ACT.Copy).then_inc(s_tab2, 1)
            nc.scalar.activation(rank_bf[:, :], rank_of[:, :], ACT.Copy).then_inc(s_tab2, 1)

            def make_mask(i, q, s):
                n = pos(i, q, s)
                early = isinstance(n, int) and n < 2
                act.wait_ge(s_adj[par(q, s)], 16 * nth(i, q, s))
                if not early:
                    act.wait_ge(s_mT, n - 1)
                nc.scalar.activation(mask[:, par(q, s)], adj_sb[:, par(q, s)], ACT.Sign).then_inc(s_mask, 1)

            def copy_maskT(i, q, s):
                n = pos(i, q, s)
                early = isinstance(n, int) and n < 2
                act.wait_ge(s_mT, n + 1)
                if not early:
                    act.wait_ge(s_Vp, 2 * (n - 1))
                    act.wait_ge(s_cnt, n - 1)
                nc.scalar.activation(maskT[:, par(q, s)], p_maskT[:, :], ACT.Square).then_inc(s_mTc, 1)

            def copy_V(i, q, s, h):
                n = pos(i, q, s)
                act.wait_ge(s_Vp, 2 * n + h + 1)
                if not (isinstance(n, int) and n < 2 * MT):
                    act.wait_ge(s_agg, n - 2 * MT + 1)
                nc.scalar.activation(V[:, q, s - 1, 4 * h:4 * h + 4], p_V[:, :].rearrange("p (b i) -> p b i", i=P),
                                     ACT.Copy).then_inc(s_V, 1)

            def after(i, q, s):
                if s < MT:
                    return (i, q, s + 1)
                if q == 0:
                    return (i, 1, 1)
                return (i + 1, 0, 1)

            def prologue():
                make_mask(0, 0, 1)
                for s in range(1, NT):
                    copy_maskT(0, 0, s)
                    make_mask(*after(0, 0, s))
                    copy_V(0, 0, s, 0)
                    copy_V(0, 0, s, 1)

            def step(i, q, last):
                ni, nq = (i, 1) if q == 0 else (i + 1, 0)
                for s in range(1, NT):
                    m = pos(i, q, s)
                    end = isinstance(ni, int) and ni == B // 2 - 1 and nq == 1 and s == MT
                    if not last:
                        copy_maskT(ni, nq, s)
                    if s == 4:
                        act.wait_ge(s_agg0t, 2 * i + q + 1)
                        nc.scalar.activation(agg0_t[:, :], p_xt, ACT.Copy).then_inc(s_agg0c, 1)
                    if s == 5:
                        act.wait_ge(s_x0t, 2 * i + q + 1)
                        nc.scalar.activation(x0_t[:, :], p_xt, ACT.Copy).then_inc(s_x0c, 1)
                    if not last and not end:
                        make_mask(*after(ni, nq, s))
                    if not last:
                        copy_V(ni, nq, s, 0)
                    act.wait_ge(s_xt, m + 1)
                    if not (isinstance(m, int) and m < 2):
                        act.wait_ge(s_out, m - 1)
                    nc.scalar.activation(xt_sb[:, par(q, s)], p_xt, ACT.Copy).then_inc(s_xtc, 1)
                    if not last:
                        copy_V(ni, nq, s, 1)
                    if s == 2 and not (isinstance(m, int) and m < MT):
                        deviation(2 * i + q - 1, 1 - q)

            def deviation(batch, q):
                act.wait_ge(s_var, batch + 1)
                nc.scalar.activation(std[:, q], mv[:, q, :, 1:2].rearrange("p t a -> p (t a)"), ACT.Sqrt,
                                     bias=eps[:, 0:1]).then_inc(s_std, 1)

            prologue()
            step(0, 0, False)
            step(0, 1, False)
            with act.Fori(1, B // 2 - 1) as i:
                step(i, 0, False)
                step(i, 1, False)
            step(B // 2 - 1, 0, False)
            step(B // 2 - 1, 1, True)
            deviation(B - 1, 1)

        @block.vector
        def _(dve):
            def one_hots(i, q, s):
                u = par(q, s)
                m = pos(i, q, s)
                if not (isinstance(m, int) and m < 2):
                    dve.wait_ge(s_pair, STATIC * (m - 1))
                dve.wait_ge(s_V, 2 * m + 2)
                for r in range(DEPTH[0][0]):
                    last = dve.tensor_scalar(hot0[:, u, r], V[:, q, s - 1, 0], float(r + 1 - MARK), None, ALU.is_equal)
                for r in range(DEPTH[0][1]):
                    last = dve.tensor_scalar(hot[:, u, :, r], V[:, q, s - 1, 1:NT], float(r + 1 - MARK), None,
                                             ALU.is_equal)
                last.then_inc(s_hot, 1)

            def reduce_pair(i, q, s, p):
                m = pos(i, q, s)
                dve.wait_ge(s_pair, STATIC * m + p + 1)
                src = half[:, :, :].rearrange("f k i -> f i k") if p == STATIC - 1 else \
                    pairs[p % 2][:, :, :, :].rearrange("f a k i -> f i (a k)")
                dve.tensor_reduce(part[:, par(q, s), p], src, AX.X, ALU.max).then_inc(s_used, 1)

            def extra_level(i, q, s, e):
                m = pos(i, q, s)
                for r in range(2):
                    dve.tensor_scalar(hotx[:, e - 1, 0, r], V[:, q, s - 1, 0],
                                      float(DEPTH[e - 1][0] + r + 1 - MARK), None, ALU.is_equal)
                    last = dve.tensor_scalar(hotx[:, e - 1, 1:NT, r], V[:, q, s - 1, 1:NT],
                                             float(DEPTH[e - 1][1] + r + 1 - MARK), None, ALU.is_equal)
                last.then_inc(s_hotx, 1)
                for p in range(EXTRA):
                    dve.wait_ge(s_xpair, 2 * EXTRA * m + EXTRA * (e - 1) + p + 1)
                    dve.tensor_reduce(more[:, :], pairs[p][:, :, :, :].rearrange("f a k i -> f i (a k)"),
                                      AX.X, ALU.max).then_inc(s_xused, 1)
                    dve.drain()
                    dve.tensor_tensor(part[:, par(q, s), 0], part[:, par(q, s), 0], more[:, :], ALU.max)
                    dve.drain()

            def extraction(w, batch, steps, bp):
                for st in steps:
                    if st == 0:
                        dve.scalar_tensor_tensor(out=g_score[w][:, :], in0=g_adj[w][:, :], scalar=0.0,
                                                 in1=falling[:, :], op0=ALU.not_equal, op1=ALU.mult
                                                 ).then_inc(s_score0 if w == 0 else s_fstep, 1)
                    elif st < 2 * ROUNDS:
                        r = (st - 1) // 2
                        val = g_val[w][:, RANKS8 * r:RANKS8 * (r + 1)]
                        if st % 2:
                            dve.max(val, g_score[w][:, :])
                        else:
                            dve.match_replace(g_score[w][:, :], val, g_score[w][:, :], 0.0)
                    else:
                        val, pick = g_val[w], g_pick[w]
                        dve.scalar_tensor_tensor(out=pick[:, :], in0=val[:, 0:K], scalar=0.0,
                                                 in1=val[:, 0:1].to_broadcast([P, K]),
                                                 op0=ALU.is_equal, op1=ALU.mult)
                        dve.tensor_scalar(g_bound[w][:, bp, 0:1], val[:, K:K + 1], 0.0, -BIG, ALU.is_gt, ALU.mult)
                        dve.tensor_scalar(g_bound[w][:, bp, 1:2], val[:, 0:1], 0.0, None, ALU.is_gt)
                        dve.drain()
                        dve.tensor_tensor(pick[:, :], pick[:, :], val[:, 0:K], ALU.max)
                        dve.drain()
                        dve.tensor_scalar(pick[:, :], pick[:, :], 1.0, None, ALU.max)
                        dve.drain()
                        dve.scalar_tensor_tensor(out=g_idx[w][:, :], in0=pick[:, :], scalar=-1.0,
                                                 in1=row_base[:, bass.ds(batch, 1)].to_broadcast([P, K]),
                                                 op0=ALU.mult, op1=ALU.add
                                                 ).then_inc(s_idx0 if w == 0 else s_fidx, 1)
                    dve.drain()

            LAST_STEP = 2 * ROUNDS

            def gathered_max(w, bp, signal):
                dve.tensor_reduce(g_max[w][:, :], g_feat[w][:, :, :].rearrange("p k f -> p f k"), AX.X,
                                  ALU.max).then_inc(s_g0max if w == 0 else s_fstep, 1)
                dve.drain()
                dve.tensor_scalar(g_agg[w][:, :], g_max[w][:, :], g_bound[w][:, bp, 0:1], g_bound[w][:, bp, 1:2],
                                  ALU.max, ALU.mult).then_inc(signal, 1)

            def redo(i, q, s):
                m = pos(i, q, s)
                dve.wait_ge(s_fadj, m + 1)
                extraction(1, 2 * i + q, range(LAST_STEP + 1), 0)
                dve.wait_ge(s_fg, m + 1)
                gathered_max(1, 0, s_fagg)
                dve.wait_ge(s_ft, m + 1)
                for p in range(STATIC):
                    dve.tensor_copy(part[:, par(q, s), p], p_xt)

            def count_violations(i, q):
                dve.wait_ge(s_cnt, MT * (2 * i + q + 1))
                n = MT * NT
                cnt = p_cnt.rearrange("p (o n) -> p o n", o=1).to_broadcast([P, LEVELS, n])
                dve.tensor_tensor(viol[:, 0:LEVELS * n].rearrange("p (l n) -> p l n", n=n), cnt,
                                  depth_tab[:, :, :, :].rearrange("p l t b -> p l (t b)"), ALU.is_gt)
                dve.tensor_reduce(degree[:, :], p_cnt.rearrange("p (t b) -> p t b", b=NT), AX.X, ALU.add)
                dve.drain()
                dve.tensor_scalar(viol[:, LEVELS * n:NV], degree[:, :], float(K), None, ALU.is_gt).then_inc(s_viol, 1)

            def set_levels(i, q):
                n = LEVELS * MT
                dve.wait_ge(s_vp, 2 * i + q + 1)
                dve.tensor_reduce(vsum[:, :], p_viol[:, 0:n * NT].rearrange("p (n b) -> p n b", b=NT), AX.X, ALU.add)
                dve.tensor_scalar(vdeg[:, :], p_viol[:, n * NT:NV], 1.0, float(LEVELS), ALU.min, ALU.mult)
                dve.drain()
                dve.tensor_scalar(vsum[:, :], vsum[:, :], 1.0, None, ALU.min)
                dve.drain()
                dve.tensor_tensor(vlow[:, :], vsum[:, 0:MT], vsum[:, MT:2 * MT], ALU.add)
                dve.scalar_tensor_tensor(out=vhigh[:, :], in0=vsum[:, 2 * MT:3 * MT], scalar=float(LEVELS),
                                         in1=vdeg[:, :], op0=ALU.mult, op1=ALU.max)
                dve.drain()
                dve.tensor_tensor(level[:, q], vlow[:, :], vhigh[:, :], ALU.max).then_inc(s_level, 1)
                dve.drain()

            def residual(i, q, t, order):
                if t == 0:
                    dve.wait_ge(s_out0, 2 * i + q + 1)
                else:
                    dve.wait_ge(s_out, pos(i, q, t) + 1)
                dve.scalar_tensor_tensor(out=y_sb[:, q, t], in0=p_out, scalar=0.0, in1=x_sb[:, q, t],
                                         op0=ALU.max, op1=ALU.add).then_inc(s_y, 1)

            def row_stats(i, q, t):
                dve.wait_ge(s_y, NT * (2 * i + q) + ORDER[t] + 1)
                dve.bn_stats(stats[:, q, t], y_sb[:, q, t])

            def variance(q):
                dve.drain()
                for t in range(NT):
                    last = dve.bn_aggr(mv[:, q, t], stats[:, q, t])
                last.then_inc(s_var, 1)

            def normalise(batch, q):
                dve.wait_ge(s_std, batch + 1)
                dve.reciprocal(rstd[:, q], std[:, q])
                dve.drain()
                for t in range(NT):
                    last = dve.tensor_scalar(y_sb[:, q, t], y_sb[:, q, t], mv[:, q, t, 0:1], rstd[:, q, t:t + 1],
                                             ALU.subtract, ALU.mult)
                last.then_inc(s_norm, 1)

            EXTRACT = {1: range(0, 2), 2: range(2, 4), 3: range(4, 6), 4: range(6, LAST_STEP + 1)}

            def step(i, q, last):
                ni, nq = (i, 1) if q == 0 else (i + 1, 0)
                pi, pq = (i, 0) if q == 1 else (i - 1, 1)
                begin = isinstance(i, int) and i == 0 and q == 0
                for s in range(1, NT):
                    m = pos(i, q, s)
                    if s == 1:
                        count_violations(i, q)
                    if s < MT:
                        one_hots(i, q, s + 1)
                    elif not last:
                        one_hots(ni, nq, 1)
                    reduce_pair(i, q, s, 0)
                    if s == 1:
                        set_levels(i, q)
                    if not last and s in EXTRACT:
                        if s == 1:
                            dve.wait_ge(s_adj0, 16 * (2 * i + q + 2))
                        extraction(0, 2 * i + q + 1, EXTRACT[s], nq)
                    reduce_pair(i, q, s, 1)
                    if s > 1:
                        if s == 2 and not (isinstance(i, int) and i == 0):
                            dve.wait_ge(s_store[q], 16 * i)
                        residual(i, q, s - 1, s - 2)
                    elif not begin:
                        residual(pi, pq, MT, MT)
                    reduce_pair(i, q, s, 2)
                    if s > 1:
                        row_stats(i, q, s - 1)
                    elif not begin:
                        row_stats(pi, pq, MT)
                    reduce_pair(i, q, s, 3)
                    if s == 6:
                        residual(i, q, 0, MT - 1)
                        row_stats(i, q, 0)
                    reduce_pair(i, q, s, 4)
                    if s == 1 and not begin:
                        variance(pq)
                    if s == 3 and not begin:
                        normalise(2 * i + q - 1, pq)
                    if s == 1:
                        dve.wait_ge(s_level, 2 * i + q + 1)
                        dve.nop(nofuse=True)
                    lv = dve.value_load(level[0:1, q, s - 1:s], min_val=0, max_val=LEVELS)
                    with dve.If(lv > 0):
                        dve.drain()
                        with dve.If(lv < LEVELS):
                            extra_level(i, q, s, 1)
                            with dve.If(lv > 1):
                                extra_level(i, q, s, 2)
                            with dve.Else():
                                dve.sem_inc(s_hotx, 1)
                                dve.sem_inc(s_xused, EXTRA)
                            dve.sem_inc(s_fidx, 1)
                            dve.sem_inc(s_fagg, 1)
                        with dve.Else():
                            redo(i, q, s)
                            dve.sem_inc(s_hotx, 2)
                            dve.sem_inc(s_xused, 2 * EXTRA)
                    with dve.Else():
                        dve.sem_inc(s_hotx, 2)
                        dve.sem_inc(s_xused, 2 * EXTRA)
                        dve.sem_inc(s_fidx, 1)
                        dve.sem_inc(s_fagg, 1)
                    dve.drain()
                    dve.tensor_reduce(agg_t[:, par(q, s)], part[:, par(q, s)].rearrange("f k i -> f i k"), AX.X,
                                      ALU.max).then_inc(s_agg, 1)
                    if s == 3:
                        dve.wait_ge(s_g0, 16 * K * (2 * i + q + 1))
                        gathered_max(0, q, s_agg0)

            dve.wait_ge(s_tab, 6 + 2 * LEVELS)
            dve.wait_ge(s_adj0, 16)
            extraction(0, 0, range(LAST_STEP + 1), 0)
            one_hots(0, 0, 1)
            step(0, 0, False)
            step(0, 1, False)
            with dve.Fori(1, B // 2 - 1) as i:
                step(i, 0, False)
                step(i, 1, False)
            step(B // 2 - 1, 0, False)
            step(B // 2 - 1, 1, True)
            residual(B // 2 - 1, 1, MT, MT)
            row_stats(B // 2 - 1, 1, MT)
            variance(1)
            normalise(B - 1, 1)

        @block.tensor
        def _(pe):
            def transpose_mask(i, q, s):
                n = pos(i, q, s)
                pe.wait_ge(s_mask, n + 1)
                if not (isinstance(n, int) and n < 1):
                    pe.wait_ge(s_mTc, n)
                for kb in range(NT):
                    last = pe.transpose(p_maskT[:, kb * P:(kb + 1) * P], mask[:, par(q, s), kb * P:(kb + 1) * P],
                                        ident_bf[:, :])
                last.then_inc(s_mT, 1)

            def rank_product(i, q, s, h, m=None):
                n = pos(i, q, s)
                if h == 0:
                    pe.wait_ge(s_mTc, n + 1)
                if not (isinstance(n, int) and 2 * n + h < 1):
                    pe.wait_ge(s_V, 2 * n + h)
                if m is not None and (h == 1 or not (isinstance(m, int) and m == 0)):
                    pe.wait_ge(s_xtc, m + h)
                pe.matmul(p_V[:, :], rank_bf[:, :], maskT[:, par(q, s), h * N // 2:(h + 1) * N // 2],
                          start=True, stop=True).then_inc(s_Vp, 1)

            def count(i, q, s):
                n = pos(i, q, s)
                if s == 1 and not (isinstance(n, int) and n < 1):
                    pe.wait_ge(s_viol, 2 * i + q)
                pe.wait_ge(s_mTc, n + 1)
                for kb in range(NT):
                    c = (s - 1) * NT + kb
                    last = pe.matmul(p_cnt[:, c:c + 1], maskT[:, par(q, s), kb * P:(kb + 1) * P], ones_bf[:, :],
                                     start=True, stop=True)
                last.then_inc(s_cnt, 1)

            def pick(dst, q, kb, one_hot, signal=None):
                for part_no in range(3):
                    last = pe.matmul(dst, x_part[:, q, part_no, kb], one_hot, start=(part_no == 0),
                                     stop=(part_no == 2))
                if signal is not None:
                    last.then_inc(signal, 1)

            def pick_pair(i, q, s, p):
                m = pos(i, q, s)
                u = par(q, s)
                start = isinstance(m, int) and m == 0
                if p == 0:
                    pe.wait_ge(s_hot, m + 1)
                    if not start:
                        pe.wait_ge(s_xused, 2 * EXTRA * m)
                if p == STATIC - 1:
                    if not start:
                        pe.wait_ge(s_used, STATIC * m)
                    pick(half[:, :, :], q, NT - 1, hot[:, u, NT - 2], s_pair)
                    return
                if p >= 2:
                    pe.wait_ge(s_used, STATIC * m + p - 1)
                elif not start:
                    pe.wait_ge(s_used, STATIC * m + p - 2)
                if p == 0:
                    pick(pairs[0][:, 0], q, 0, hot0[:, u, 0:4])
                    pick(pairs[0][:, 1], q, 0, hot0[:, u, 4:8], s_pair)
                else:
                    pick(pairs[p % 2][:, 0], q, 2 * p - 1, hot[:, u, 2 * p - 2])
                    pick(pairs[p % 2][:, 1], q, 2 * p, hot[:, u, 2 * p - 1], s_pair)

            def extra_level(i, q, s, e):
                m = pos(i, q, s)
                pe.wait_ge(s_hotx, 2 * m + e)
                for p in range(EXTRA):
                    if e == 1:
                        pe.wait_ge(s_used, STATIC * m + 3 + p)
                    else:
                        pe.wait_ge(s_xused, 2 * EXTRA * m + p + 1)
                    for j in range(4):
                        kb = 4 * p + j
                        pick(pairs[p][:, j // 2, 2 * (j % 2):2 * (j % 2) + 2], q, kb, hotx[:, e - 1, kb],
                             s_xpair if j == 3 else None)

            def turn_features(q, t, signal):
                for part_no in range(3):
                    last = pe.matmul(p_xt, x_part[:, q, part_no, t], ident_bf[:, :], start=(part_no == 0),
                                     stop=(part_no == 2))
                last.then_inc(signal, 1)

            def transpose_x(i, q, s, vcopies):
                m = pos(i, q, s)
                if not (isinstance(m, int) and m == 0):
                    pe.wait_ge(s_xtc, m)
                pe.wait_ge(s_V, vcopies)
                turn_features(q, s, s_xt)

            def linear(xt, agg, signal):
                pe.matmul(p_out, xt, w_sb[:, 0], start=True, stop=False)
                pe.matmul(p_out, agg, w_sb[:, 1], start=False, stop=False)
                pe.matmul(p_out, ones_row[:, :], bias[:, :], start=False, stop=True).then_inc(signal, 1)

            def out_free(i, q, order):
                if not (isinstance(i, int) and i == 0 and q == 0 and order <= 0):
                    pe.wait_ge(s_y, NT * (2 * i + q) + order)

            def linear_main(i, q, s):
                m = pos(i, q, s)
                out_free(i, q, ORDER[s])
                pe.wait_ge(s_xtc, m + 1)
                pe.wait_ge(s_agg, m + 1)
                linear(xt_sb[:, par(q, s)], agg_t[:, par(q, s)], s_out)

            def violations(i, q):
                pe.wait_ge(s_viol, 2 * i + q + 1)
                pe.matmul(p_viol, ones_bf[:, :], viol[:, :], start=True, stop=True).then_inc(s_vp, 1)

            def step(i, q, last):
                ni, nq = (i, 1) if q == 0 else (i + 1, 0)
                pi, pq = (i, 0) if q == 1 else (i - 1, 1)
                begin = isinstance(i, int) and i == 0 and q == 0
                for s in range(1, NT):
                    m = pos(i, q, s)
                    if s == 1:
                        pe.wait_ge(s_split, 2 * i + q + 1)
                    vc = 2 * pos(ni, nq, s) if not last else 2 * MAIN
                    pick_pair(i, q, s, 0)
                    if s == 1:
                        violations(i, q)
                    if not last:
                        transpose_mask(ni, nq, s)
                    pick_pair(i, q, s, 1)
                    if s == 4:
                        pe.wait_ge(s_xtc, m)
                        pe.wait_ge(s_V, vc)
                        pe.wait_ge(s_agg0, 2 * i + q + 1)
                        pe.transpose(p_xt, g_agg[0][:, :], ident[:, :]).then_inc(s_agg0t, 1)
                    if s == 5:
                        pe.wait_ge(s_xtc, m)
                        pe.wait_ge(s_V, vc)
                        turn_features(q, 0, s_x0t)
                    if s == 1:
                        pe.wait_ge(s_level, 2 * i + q + 1)
                    if not (begin and s == 1):
                        out_free(i, q, ORDER[s - 1] if s > 1 else -1)
                    if not last:
                        count(ni, nq, s)
                    if s > 1:
                        linear_main(i, q, s - 1)
                    elif not begin:
                        linear_main(pi, pq, MT)
                    pick_pair(i, q, s, 2)
                    if s == 4:
                        pe.wait_ge(s_agg0c, 2 * i + q + 1)
                    if s == 5:
                        pe.wait_ge(s_x0c, 2 * i + q + 1)
                    if not last:
                        rank_product(ni, nq, s, 0, m)
                    pick_pair(i, q, s, 3)
                    transpose_x(i, q, s, vc + 1 if not last else vc)
                    if s == 6:
                        out_free(i, q, ORDER[0])
                        linear(x0_t[:, :], agg0_t[:, :], s_out0)
                    pick_pair(i, q, s, 4)
                    if not last:
                        rank_product(ni, nq, s, 1, m)
                    if s == 1:
                        pe.wait_ge(s_level, 2 * i + q + 1)
                        pe.nop(nofuse=True)
                    lv = pe.value_load(level[0:1, q, s - 1:s], min_val=0, max_val=LEVELS)
                    with pe.If(lv > 0):
                        with pe.If(lv < LEVELS):
                            extra_level(i, q, s, 1)
                            with pe.If(lv > 1):
                                extra_level(i, q, s, 2)
                            with pe.Else():
                                pe.wait_ge(s_xused, 2 * EXTRA * m + EXTRA)
                                pe.sem_inc(s_xpair, EXTRA)
                            pe.sem_inc(s_ft, 1)
                        with pe.Else():
                            pe.sem_inc(s_xpair, 2 * EXTRA)
                            pe.wait_ge(s_fagg, m + 1)
                            pe.wait_ge(s_xtc, m + 1)
                            pe.wait_ge(s_V, vc + 2 if not last else vc)
                            pe.transpose(p_xt, g_agg[1][:, :], ident[:, :]).then_inc(s_ft, 1)
                            pe.wait_ge(s_agg, m + 1)
                    with pe.Else():
                        pe.sem_inc(s_xpair, 2 * EXTRA)
                        pe.sem_inc(s_ft, 1)

            pe.wait_ge(s_tab, 6 + 2 * LEVELS)
            pe.wait_ge(s_tab2, 2)
            for s in range(1, NT):
                transpose_mask(0, 0, s)
                rank_product(0, 0, s, 0)
                count(0, 0, s)
                rank_product(0, 0, s, 1)
            pe.wait_ge(s_const, 32)
            step(0, 0, False)
            step(0, 1, False)
            with pe.Fori(1, B // 2 - 1) as i:
                step(i, 0, False)
                step(i, 1, False)
            step(B // 2 - 1, 0, False)
            step(B // 2 - 1, 1, True)
            linear_main(B // 2 - 1, 1, MT)


def kernel(x, adj, L0_gnn_W, L0_gnn_b):
    import numpy as np
    import concourse.bacc as bacc
    from concourse.bass_utils import run_bass_kernel_spmd as run

    nc = bacc.Bacc("TRN2", target_bir_lowering=False, num_devices=1)
    arrays, args = {}, []
    for name, a in (("x", x), ("adj", adj), ("W", L0_gnn_W), ("b", L0_gnn_b)):
        a = np.ascontiguousarray(a)
        arrays["in_" + name] = a
        args.append(nc.dram_tensor("in_" + name, a.shape, mybir.dt.from_np(a.dtype), kind="ExternalInput").ap())
    out = nc.dram_tensor("out", x.shape, F32, kind="ExternalOutput").ap()
    build(nc, *args, out)
    r = run(nc, [arrays], core_ids=[0])
    return r.results[0]["out"]
```

```python
import concourse.bass as bass
from concourse import mybir
from contextlib import ExitStack

F32 = mybir.dt.float32
BF16 = mybir.dt.bfloat16
I32 = mybir.dt.int32
ALU = mybir.AluOpType
ACT = mybir.ActivationFunctionType
AX = mybir.AxisListType

P = 128
K = 25
EPS = 1e-5
BIG = 3.0e38
MARK = 256
RANKS8 = 8
ROUNDS = -(-(K + 1) // RANKS8)
LAST_STEP = 2 * ROUNDS
BANK = 4
DEPTHS = {1: (12, 7, 6, 6, 6, 5, 5, 5),
          2: (9, 6, 5, 5, 5, 5, 5, 4), 3: (9, 6, 5, 5, 5, 5, 5, 4),
          4: (7, 5, 4, 4, 4, 4, 4, 4), 5: (7, 5, 4, 4, 4, 4, 4, 4),
          6: (7, 5, 4, 4, 4, 4, 4, 4), 7: (7, 5, 4, 4, 4, 4, 4, 4)}
DEEPER = 2
LOW = 6
HIGH_BLOCKS = 2
ACT_RANKS = 2


def banks(depths):
    pieces = []
    for kb, d in enumerate(depths):
        pieces += [(kb, r, min(BANK, d - r)) for r in range(0, d, BANK)]
    pieces.sort(key=lambda piece: -piece[2])
    filled = []
    for kb, r, n in pieces:
        for bank in filled:
            used = sum(piece[2] for piece in bank)
            if used + n <= BANK:
                break
        else:
            bank, used = [], 0
            filled.append(bank)
        for a, z in ((r, min(r + n, LOW)), (max(r, LOW), r + n)):
            if a < z:
                bank.append((kb, a, z - a, used + a - r))
    return filled


def build(nc, x, adj, W, b, out):
    B, N, C = x.shape
    NT = N // P
    MT = NT - 1
    MAIN = B * MT
    EXTRA = NT * DEEPER // (2 * BANK)
    LEVELS = 2
    BANKS = {s: banks(DEPTHS[s]) for s in range(1, NT)}
    PAIRS = {s: len(BANKS[s]) // 2 for s in range(1, NT)}
    FIRST = {s: sum(PAIRS[t] for t in range(1, s)) for s in range(1, NT)}
    BATCH_PAIRS = sum(PAIRS.values())
    MAX_PAIRS = max(PAIRS.values())
    RANKS = max(d[0] for d in DEPTHS.values())
    assert all(sum(piece[2] for piece in bank) == BANK for s in BANKS for bank in BANKS[s])
    assert all(len(BANKS[s]) % 2 == 1 for s in BANKS) and BATCH_PAIRS % 2 == 0
    assert all(d[HIGH_BLOCKS] <= LOW and list(d) == sorted(d, reverse=True) for d in DEPTHS.values())
    KINDS = [[t for t in DEPTHS if DEPTHS[t] == d] for d in sorted(set(DEPTHS.values()), reverse=True)]

    def runs(depths):
        starts = [kb for kb in range(NT) if kb == 0 or depths[kb] != depths[kb - 1]]
        return list(zip(starts, starts[1:] + [NT]))
    TABLES = 8 + sum(len(runs(DEPTHS[kind[0]])) for kind in KINDS)

    x_rows = x.rearrange("b n c -> (b n) c")
    x_tiles = x.rearrange("b (t p) c -> b p t c", p=P)
    out_tiles = out.rearrange("b (t p) c -> b p t c", p=P)
    adj_tiles = adj.rearrange("b (t p) n -> (b t) p n", p=P)

    ctx = ExitStack()
    with ctx:
        def sb(name, shape, dt):
            return ctx.enter_context(nc.sbuf_tensor(name, shape, dt))

        def psum(name, shape, dt):
            return ctx.enter_context(nc.psum_tensor(name, shape, dt))

        def sem(name):
            return ctx.enter_context(nc.semaphore(name))

        w_sb = sb("w_sb", [P, 2, C], F32)
        bias = sb("bias", [1, C], F32)
        ones_row = sb("ones_row", [1, P], F32)
        ones_bf = sb("ones_bf", [P, 1], BF16)
        eps = sb("eps", [P, 1], F32)
        first_bias = sb("first_bias", [P, 1], F32)
        second_bias = sb("second_bias", [P, 1], F32)
        one = sb("one", [P, 1], F32)
        falling = sb("falling", [P, N], F32)
        row_base = sb("row_base", [P, B], F32)
        iota_work = sb("iota_work", [P, P], F32)
        ident = sb("ident", [P, P], F32)
        ident_bf = sb("ident_bf", [P, P], BF16)
        rank_of = sb("rank_of", [P, P], F32)
        rank_bf = sb("rank_bf", [P, P], BF16)
        depth_tab = sb("depth_tab", [P, LEVELS, MT, NT], F32)
        x_sb = sb("x_sb", [P, 2, NT, C], F32)
        x_part = sb("x_part", [P, 2, 3, NT, C], BF16)
        x_rest = sb("x_rest", [P, NT, C], F32)
        adj_sb = sb("adj_sb", [P, 2, N], I32)
        mask = sb("mask", [P, 2, N], BF16)
        maskT = sb("maskT", [P, 2, N], BF16)
        V = sb("V", [P, 2, MT, NT, P], BF16)
        hot = sb("hot", [P, 2, LOW, NT, P], BF16)
        hot_high = sb("hot_high", [P, 2, RANKS - LOW, HIGH_BLOCKS, P], BF16)
        distance = sb("distance", [P, NT, P], BF16)
        hotx = sb("hotx", [P, DEEPER, NT, P], BF16)
        viol = sb("viol", [P, LEVELS, MT, NT + 1], BF16)
        degree = sb("degree", [P, MT], F32)
        vsum = sb("vsum", [1, LEVELS, MT], F32)
        level = sb("level", [1, 2, MT], I32)
        part = sb("part", [P, 2, BANK + MAX_PAIRS, P], F32)
        more = sb("more", [P, EXTRA, P], F32)
        agg_t = sb("agg_t", [P, 2, P], F32)
        xt_sb = sb("xt_sb", [P, 2, P], F32)
        g_adj = [sb(f"g_adj{w}", [P, N], I32) for w in range(2)]
        g_score = [sb(f"g_score{w}", [P, N], F32) for w in range(2)]
        g_val = [sb(f"g_val{w}", [P, RANKS8 * ROUNDS], F32) for w in range(2)]
        g_pick = [sb(f"g_pick{w}", [P, K], F32) for w in range(2)]
        g_bound = [sb(f"g_bound{w}", [P, 2, 2], F32) for w in range(2)]
        g_idx = [sb(f"g_idx{w}", [P, K], I32) for w in range(2)]
        g_feat = [sb(f"g_feat{w}", [P, K, C], F32) for w in range(2)]
        g_max = [sb(f"g_max{w}", [P, C], F32) for w in range(2)]
        g_agg = [sb(f"g_agg{w}", [P, C], F32) for w in range(2)]
        agg0_t = sb("agg0_t", [P, P], F32)
        x0_t = sb("x0_t", [P, P], F32)
        y_sb = sb("y_sb", [P, 2, NT, C], F32)
        relu_sb = sb("relu_sb", [P, 2, C], F32)
        row_work = sb("row_work", [P, NT, C], F32)
        mean_neg = sb("mean_neg", [P, 2, NT], F32)
        square_sum = sb("square_sum", [P, 2, NT], F32)
        std = sb("std", [P, 2, NT], F32)
        rstd = sb("rstd", [P, 2, NT], F32)
        shift = sb("shift", [P, 2, NT], F32)

        pairs = [psum(f"pair{i}", [P, 2, 4, P], F32) for i in range(2)]
        half = psum("half", [P, 4, P], F32)
        p_maskT = psum("p_maskT", [P, N], BF16)
        p_V = psum("p_V", [P, N // 2], F32)
        misc = psum("misc", [P, 512], F32)
        p_out = misc[:, 0:C]
        p_xt = p_V[:, 0:P]
        p_cnt = misc[:, P:P + MT * NT]
        NV = LEVELS * MT * (NT + 1)
        p_viol = misc[0:1, 2 * P:2 * P + NV]

        s_const = sem("weights_loaded")
        s_tab = sem("tables_ready")
        s_ptab = sem("pool_table_step")
        s_falling = sem("falling_scores_ready")
        s_tab2 = sem("bf16_tables_ready")
        s_x = [sem(f"x_loaded{q}") for q in range(2)]
        s_high = sem("x_high_ready")
        s_rest = sem("x_rest_ready")
        s_mid = sem("x_mid_ready")
        s_split = sem("x_split_ready")
        s_adj = [sem(f"adj_loaded{u}") for u in range(2)]
        s_mask = sem("mask_ready")
        s_mT = sem("mask_transposed")
        s_mTc = sem("maskT_ready")
        s_Vp = sem("V_product")
        s_V = sem("V_ready")
        s_cnt = sem("counts_ready")
        s_viol = sem("violations_ready")
        s_vp = sem("violations_summed")
        s_level = sem("level_ready")
        s_hot = sem("onehots_ready")
        s_pair = sem("picked")
        s_used = sem("picked_reduced")
        s_half = sem("half_picked")
        s_halfc = sem("half_copied")
        s_hotx = sem("extra_onehots_ready")
        s_xpair = sem("extra_picked")
        s_xused = sem("extra_reduced")
        s_xdone = sem("extra_merged")
        s_agg = sem("agg_ready")
        s_xt = sem("x_transposed")
        s_xtc = sem("xT_ready")
        s_out = sem("linear_done")
        s_y = sem("residual_added")
        s_relu = sem("relu_ready")
        s_mean = sem("means_ready")
        s_square = sem("squares_summed")
        s_hot1 = sem("first_rank_onehots_ready")
        s_hot2 = sem("second_rank_onehots_ready")
        s_distance = sem("distances_ready")
        s_std = sem("std_ready")
        s_affine = sem("scale_shift_ready")
        s_norm = sem("normalised")
        s_store = [sem(f"stored{q}") for q in range(2)]
        s_ex = sem("extraction0_step")
        s_adj0 = sem("adj0_loaded")
        s_idx0 = sem("idx0_ready")
        s_g0 = sem("gathered0")
        s_g0max = sem("gathered0_reduced")
        s_agg0 = sem("agg0_ready")
        s_agg0t = sem("agg0_transposed")
        s_agg0c = sem("agg0T_ready")
        s_x0t = sem("x0_transposed")
        s_x0c = sem("x0T_ready")
        s_out0 = sem("linear0_done")
        s_fstep = sem("redo_step")
        s_fdma = sem("redo_dma")
        s_fadj = sem("redo_adj_ready")
        s_fidx = sem("redo_idx_ready")
        s_fg = sem("redo_gathered")
        s_fagg = sem("redo_agg_ready")
        s_ft = sem("redo_transposed")

        def pos(i, q, s):
            return 2 * MT * i + MT * q + (s - 1)

        def par(q, s):
            return (MT * q + s - 1) % 2

        def nth(i, q, s):
            return MT * i + (MT * q + s - 1) // 2 + 1

        def pair_no(i, q, s, p):
            return 2 * BATCH_PAIRS * i + BATCH_PAIRS * q + FIRST[s] + p

        def buffer_of(s, p):
            return (FIRST[s] + p) % 2

        SEQUENCE = [*range(1, MT), 0, MT]
        ORDER = {t: SEQUENCE.index(t) for t in range(NT)}

        def run(eng, step):
            step(0, 0, False)
            step(0, 1, False)
            with eng.Fori(1, B // 2 - 1) as i:
                step(i, 0, False)
                step(i, 1, False)
            step(B // 2 - 1, 0, False)
            step(B // 2 - 1, 1, True)

        def following(i, q):
            return (i, 1) if q == 0 else (i + 1, 0)

        def preceding(i, q):
            return (i, 0) if q == 1 else (i - 1, 1)

        def is_first(i, q):
            return isinstance(i, int) and i == 0 and q == 0

        block = ctx.enter_context(nc.Block())

        @block.sync
        def _(sp):
            def load_x(i, q):
                sp.dma_start(x_sb[:, q], x_tiles[bass.ds(2 * i + q, 1)].rearrange("a p t c -> p (a t) c")
                             ).then_inc(s_x[q], 16)

            def load_adj(i, q, s):
                sp.dma_start(adj_sb[:, par(q, s)], adj_tiles[bass.ds(2 * NT * i + NT * q + s, 1)]
                             .rearrange("a p n -> p (a n)")).then_inc(s_adj[par(q, s)], 16)

            def load_adj0(i, q):
                sp.dma_start(g_adj[0][:, :], adj_tiles[bass.ds(2 * NT * i + NT * q, 1)]
                             .rearrange("a p n -> p (a n)")).then_inc(s_adj0, 16)

            def store(i, q):
                sp.wait_ge(s_norm, NT * (2 * i + q + 1))
                sp.dma_start(out_tiles[bass.ds(2 * i + q, 1)].rearrange("a p t c -> p (a t) c"),
                             y_sb[:, q]).then_inc(s_store[q], 16)

            def step(i, q, last):
                ni, nq = following(i, q)
                for s in range(1, NT):
                    if not last:
                        sp.wait_ge(s_mask, pos(ni, nq, s) - 1)
                        load_adj(ni, nq, s)
                    if s == 1 and not last:
                        sp.wait_ge(s_ex, LAST_STEP * (2 * i + q) + 1)
                        load_adj0(ni, nq)
                    if s == 2 and not last:
                        if not is_first(i, q):
                            sp.wait_ge(s_y, NT * (2 * i + q))
                        load_x(ni, nq)
                    if s == 1 and not (isinstance(i, int) and i == 0):
                        store(i - 1, q)

            load_adj0(0, 0)
            load_adj(0, 0, 1)
            load_adj(0, 0, 2)
            load_x(0, 0)
            sp.dma_start(w_sb[:, :, :], W.rearrange("(h f) o -> f h o", h=2)).then_inc(s_const, 16)
            sp.dma_start(bias[:, :], b.rearrange("(a d) -> a d", a=1)).then_inc(s_const, 16)
            for s in range(3, NT):
                sp.wait_ge(s_mask, s - 2)
                load_adj(0, 0, s)
            run(sp, step)
            store(B // 2 - 1, 0)
            for a, z in ((0, MT), (MT, NT)):
                sp.wait_ge(s_norm, NT * (B - 1) + z)
                sp.dma_start(out_tiles[B - 1, :, a:z], y_sb[:, 1, a:z]).then_inc(s_store[1], 16)
            sp.wait_ge(s_store[0], 16 * (B // 2))
            sp.wait_ge(s_store[1], 16 * (B // 2 + 1))

        @block.gpsimd
        def _(pool):
            pool.memset(ident[:, :], 0.0).then_inc(s_ptab, 1)
            pool.memset(iota_work[:, :], 1.0).then_inc(s_ptab, 1)
            pool.iota(falling[:, :], [[-1, N]], base=N, channel_multiplier=0,
                      allow_small_or_imprecise_dtypes=True).then_inc(s_falling, 1)
            pool.memset(ones_row[:, :], 1.0).then_inc(s_tab, 1)
            pool.memset(ones_bf[:, :], 1.0).then_inc(s_tab, 1)
            pool.memset(eps[:, :], EPS).then_inc(s_tab, 1)
            pool.memset(first_bias[:, :], 2.0 - MARK).then_inc(s_tab, 1)
            pool.memset(second_bias[:, :], MARK - 2.0).then_inc(s_tab, 1)
            pool.memset(one[:, :], 1.0).then_inc(s_tab, 1)
            pool.wait_ge(s_ptab, 2)
            pool.affine_select(out=ident[:, :], in_=ident[:, :], compare_op=ALU.not_equal, fill=1.0,
                               base=0, pattern=[[-1, P]], channel_multiplier=1).then_inc(s_ptab, 1)
            pool.affine_select(out=iota_work[:, :], in_=iota_work[:, :], compare_op=ALU.is_ge, fill=0.0,
                               base=0, pattern=[[1, P]], channel_multiplier=-1).then_inc(s_ptab, 1)
            pool.wait_ge(s_ptab, 4)
            pool.affine_select(out=rank_of[:, :], in_=iota_work[:, :], compare_op=ALU.not_equal,
                               fill=1.0 - MARK, base=0, pattern=[[-1, P]],
                               channel_multiplier=1).then_inc(s_ptab, 1)
            pool.iota(row_base[:, :], [[N, B]], base=N, channel_multiplier=0,
                      allow_small_or_imprecise_dtypes=True).then_inc(s_tab, 1)
            for kind in KINDS:
                depths = DEPTHS[kind[0]]
                for a, z in runs(depths):
                    pool.memset(depth_tab[:, 0, kind[0] - 1:kind[-1], a:z], float(depths[a])).then_inc(s_tab, 1)
            pool.wait_ge(s_tab, TABLES - 1)
            pool.tensor_scalar(depth_tab[:, 1], depth_tab[:, 0], float(DEEPER), None, ALU.add).then_inc(s_tab, 1)

            redone = pool.alloc_register("redone")
            pool.reg_mov(redone, 0)

            def wait(semaphore, value):
                pool.wait_ge(semaphore, value)
                pool.nop(nofuse=True)

            def split_rest(i, q):
                wait(s_high, 2 * i + q + 1)
                pool.tensor_tensor(x_rest[:, :, :], x_sb[:, q], x_part[:, q, 0], ALU.subtract).then_inc(s_rest, 1)

            def split_low(i, q):
                wait(s_mid, 2 * i + q + 1)
                pool.tensor_tensor(x_part[:, q, 2], x_rest[:, :, :], x_part[:, q, 1], ALU.subtract).then_inc(s_split, 1)

            def gather(w, signal, ks):
                for k in ks:
                    pool.indirect_dma_start(
                        out=g_feat[w][:, k, :], out_offset=None, in_=x_rows,
                        in_offset=bass.IndirectOffsetOnAxis(ap=g_idx[w][:, k:k + 1], axis=0)).then_inc(signal, 16)

            GATHER = -(-K // 5)

            def gather0(i, q, s):
                if s == 1:
                    wait(s_idx0, 2 * i + q + 1)
                    if not is_first(i, q):
                        wait(s_g0max, 2 * i + q)
                gather(0, s_g0, range(GATHER * (s - 1), min(GATHER * s, K)))

            def redo(i, q, s):
                m = pos(i, q, s)
                if s == 1:
                    wait(s_level, 2 * i + q + 1)
                lv = pool.value_load(level[0:1, q, s - 1:s], min_val=0, max_val=LEVELS)
                with pool.If(lv == LEVELS):
                    pool.dma_start(g_adj[1][:, :], adj_tiles[bass.ds(2 * NT * i + NT * q + s, 1)]
                                   .rearrange("a p n -> p (a n)")).then_inc(s_fdma, 16)
                    before = pool.snap(redone, min_val=0, max_val=MAIN * 16 * (K + 1))
                    pool.wait_ge(s_fdma, before + 16)
                    pool.sem_inc(s_fadj, 1)
                    wait(s_fidx, m + 1)
                    gather(1, s_fdma, range(K))
                    pool.wait_ge(s_fdma, before + 16 * (K + 1))
                    pool.reg_add(redone, redone, 16 * (K + 1))
                    pool.sem_inc(s_fg, 1)
                with pool.Else():
                    pool.sem_inc(s_fadj, 1)
                    pool.sem_inc(s_fg, 1)

            def residual(i, q, t):
                n = NT * (2 * i + q) + ORDER[t]
                wait(s_relu, n + 1)
                pool.tensor_tensor(y_sb[:, q, t], relu_sb[:, ORDER[t] % 2], x_sb[:, q, t], ALU.add).then_inc(s_y, 1)

            def step(i, q, last):
                ni, nq = following(i, q)
                pi, pq = preceding(i, q)
                for s in range(1, NT):
                    if s <= 5:
                        gather0(i, q, s)
                    if s > 1:
                        if s == 2 and not (isinstance(i, int) and i == 0):
                            wait(s_store[q], 16 * i)
                        residual(i, q, s - 1)
                    elif not is_first(i, q):
                        residual(pi, pq, 0)
                        residual(pi, pq, MT)
                    if s == 3 and not last:
                        split_rest(ni, nq)
                    if s == 5 and not last:
                        split_low(ni, nq)
                    redo(i, q, s)

            split_rest(0, 0)
            split_low(0, 0)
            run(pool, step)
            residual(B // 2 - 1, 1, 0)
            residual(B // 2 - 1, 1, MT)

        @block.scalar
        def _(act):

            def make_mask(i, q, s):
                n = pos(i, q, s)
                early = isinstance(n, int) and n < 2
                act.wait_ge(s_adj[par(q, s)], 16 * nth(i, q, s))
                if not early:
                    act.wait_ge(s_mT, n - 1)
                nc.scalar.activation(mask[:, par(q, s)], adj_sb[:, par(q, s)], ACT.Sign).then_inc(s_mask, 1)

            def copy_maskT(i, q, s):
                n = pos(i, q, s)
                early = isinstance(n, int) and n < 2
                act.wait_ge(s_mT, n + 1)
                if not early:
                    act.wait_ge(s_Vp, 2 * (n - 1))
                    act.wait_ge(s_cnt, n - 1)
                nc.scalar.activation(maskT[:, par(q, s)], p_maskT[:, :], ACT.Square).then_inc(s_mTc, 1)

            def copy_V(i, q, s, h):
                n = pos(i, q, s)
                act.wait_ge(s_Vp, 2 * n + h + 1)
                if not (isinstance(n, int) and n < 2 * MT):
                    act.wait_ge(s_agg, n - 2 * MT + 1)
                nc.scalar.activation(V[:, q, s - 1, 4 * h:4 * h + 4], p_V[:, :].rearrange("p (b i) -> p b i", i=P),
                                     ACT.Copy).then_inc(s_V, 1)

            def after(i, q, s):
                if s < MT:
                    return (i, q, s + 1)
                if q == 0:
                    return (i, 1, 1)
                return (i + 1, 0, 1)

            def split_high(i, q):
                act.wait_ge(s_x[q], 16 * (i + 1))
                if not (isinstance(i, int) and i == 0):
                    act.wait_ge(s_agg, MT * (2 * i + q - 1))
                nc.scalar.activation(x_part[:, q, 0], x_sb[:, q], ACT.Copy).then_inc(s_high, 1)

            def split_mid(i, q):
                act.wait_ge(s_rest, 2 * i + q + 1)
                nc.scalar.activation(x_part[:, q, 1], x_rest[:, :, :], ACT.Copy).then_inc(s_mid, 1)

            def first_rank(i, q, s):
                m = pos(i, q, s)
                act.wait_ge(s_V, 2 * m + 2)
                if not (isinstance(m, int) and m < 2):
                    act.wait_ge(s_half, m - 1)
                nc.scalar.activation(hot[:, par(q, s), 0], V[:, q, s - 1], ACT.Relu, bias=first_bias[:, 0:1],
                                     scale=-1.0).then_inc(s_hot1, 1)

            def second_distance(i, q, s):
                m = pos(i, q, s)
                if not (isinstance(m, int) and m == 0):
                    act.wait_ge(s_hot2, m)
                nc.scalar.activation(distance[:, :, :], V[:, q, s - 1], ACT.Square, bias=second_bias[:, 0:1]
                                     ).then_inc(s_distance, 1)

            def second_rank(i, q, s):
                m = pos(i, q, s)
                act.wait_ge(s_distance, m + 1)
                nc.scalar.activation(hot[:, par(q, s), 1], distance[:, :, :], ACT.Relu, bias=one[:, 0:1],
                                     scale=-1.0).then_inc(s_hot2, 1)

            def relu(i, q, t):
                n = NT * (2 * i + q) + ORDER[t]
                if t == 0:
                    act.wait_ge(s_out0, 2 * i + q + 1)
                else:
                    act.wait_ge(s_out, pos(i, q, t) + 1)
                if not (isinstance(n, int) and n < 2):
                    act.wait_ge(s_y, n - 1)
                nc.scalar.activation(relu_sb[:, ORDER[t] % 2], p_out, ACT.Relu).then_inc(s_relu, 1)

            def copy_half(i, q, s):
                m = pos(i, q, s)
                act.wait_ge(s_half, m + 1)
                if not (isinstance(m, int) and m < 2):
                    act.wait_ge(s_agg, m - 1)
                nc.scalar.activation(part[:, par(q, s), 0:BANK], half[:, :, :], ACT.Copy).then_inc(s_halfc, 1)

            def step(i, q, last):
                ni, nq = following(i, q)
                pi, pq = preceding(i, q)
                for s in range(1, NT):
                    m = pos(i, q, s)
                    end = isinstance(ni, int) and ni == B // 2 - 1 and nq == 1 and s == MT
                    if not last:
                        copy_maskT(ni, nq, s)
                    if s == 5:
                        act.wait_ge(s_x0t, 2 * i + q + 1)
                        nc.scalar.activation(x0_t[:, :], p_xt, ACT.Copy).then_inc(s_x0c, 1)
                    if not last and not end:
                        make_mask(*after(ni, nq, s))
                    act.wait_ge(s_xt, m + 1)
                    if not (isinstance(m, int) and m < 2):
                        act.wait_ge(s_out, m - 1)
                    nc.scalar.activation(xt_sb[:, par(q, s)], p_xt, ACT.Copy).then_inc(s_xtc, 1)
                    nxt = (i, q, s + 1) if s < MT else None if last else (ni, nq, 1)
                    if nxt:
                        first_rank(*nxt)
                        second_distance(*nxt)
                    if s == MT:
                        act.wait_ge(s_agg0t, 2 * i + q + 1)
                        nc.scalar.activation(agg0_t[:, :], p_xt, ACT.Copy).then_inc(s_agg0c, 1)
                    if s > 1:
                        relu(i, q, s - 1)
                    if not last:
                        copy_V(ni, nq, s, 0)
                    if nxt:
                        second_rank(*nxt)
                    if s == 1 and not is_first(i, q):
                        relu(pi, pq, MT)
                    copy_half(i, q, s)
                    if s == MT:
                        relu(i, q, 0)
                    if not last:
                        copy_V(ni, nq, s, 1)
                    if not is_first(i, q):
                        before = 2 * i + q - 1
                        if s in (2, 3):
                            means(before, pq, range(4 * (s - 2), 4 * (s - 1)))
                        if s in (4, 5):
                            squares(before, pq, range(4 * (s - 4), 4 * (s - 3)))
                        if s == 5:
                            deviation(before, pq)
                        if s in (6, 7):
                            normalise(before, pq, range(4 * (s - 6), 4 * (s - 5)))
                    if last and s == MT - 1:
                        means(B - 1, 1, range(0, 4))
                    if last and s == MT:
                        squares(B - 1, 1, range(0, 4))
                    if s == 2 and not last:
                        split_high(ni, nq)
                    if s == 4 and not last:
                        split_mid(ni, nq)

            def means(batch, q, places):
                for k in places:
                    t = SEQUENCE[k]
                    if k == places[0]:
                        act.wait_ge(s_y, NT * batch + places[-1] + 1)
                    nc.scalar.activation(row_work[:, t], y_sb[:, q, t], ACT.Copy, scale=-1.0 / C,
                                         accum_out=mean_neg[:, q, t:t + 1]).then_inc(s_mean, 1)

            def squares(batch, q, places):
                for k in places:
                    t = SEQUENCE[k]
                    if k == places[0]:
                        act.wait_ge(s_mean, NT * batch + places[-1] + 1)
                    nc.scalar.activation(row_work[:, t], y_sb[:, q, t], ACT.Square, bias=mean_neg[:, q, t:t + 1],
                                         accum_out=square_sum[:, q, t:t + 1]).then_inc(s_square, 1)

            def normalise(batch, q, places):
                act.wait_ge(s_affine, batch + 1)
                for k in places:
                    t = SEQUENCE[k]
                    nc.scalar.activation(y_sb[:, q, t], y_sb[:, q, t], ACT.Identity,
                                         bias=shift[:, q, t:t + 1], scale=rstd[:, q, t:t + 1]).then_inc(s_norm, 1)

            def deviation(batch, q, a=0, z=NT):
                act.wait_ge(s_square, NT * batch + z)
                nc.scalar.activation(std[:, q, a:z], square_sum[:, q, a:z], ACT.Sqrt, bias=eps[:, 0:1],
                                     scale=1.0 / C).then_inc(s_std, 1)

            make_mask(0, 0, 1)
            act.wait_ge(s_ptab, 5)
            nc.scalar.activation(ident_bf[:, :], ident[:, :], ACT.Copy).then_inc(s_tab2, 1)
            nc.scalar.activation(rank_bf[:, :], rank_of[:, :], ACT.Copy).then_inc(s_tab2, 1)
            make_mask(0, 0, 2)
            for s in range(1, NT):
                copy_maskT(0, 0, s)
                if s < MT:
                    make_mask(*after(0, 0, s + 1))
                if s == 1:
                    split_high(0, 0)
                if s == 4:
                    split_mid(0, 0)
            act.wait_ge(s_tab, TABLES)
            first_rank(0, 0, 1)
            second_distance(0, 0, 1)
            second_rank(0, 0, 1)
            run(act, step)
            means(B - 1, 1, range(4, MT))
            squares(B - 1, 1, range(4, MT))
            deviation(B - 1, 1, 0, MT)
            relu(B // 2 - 1, 1, MT)
            means(B - 1, 1, range(MT, NT))
            squares(B - 1, 1, range(MT, NT))
            deviation(B - 1, 1, MT, NT)

        @block.vector
        def _(dve):
            def one_hots(i, q, s, ranks, finish):
                u = par(q, s)
                m = pos(i, q, s)
                for r in ranks:
                    if r == ranks[0] == ACT_RANKS:
                        if not (isinstance(m, int) and m < 2):
                            dve.wait_ge(s_half, m - 1)
                        dve.wait_ge(s_V, 2 * m + 2)
                    blocks = sum(d > r for d in DEPTHS[s])
                    dst = hot[:, u, r, 0:blocks] if r < LOW else hot_high[:, u, r - LOW, 0:blocks]
                    last = dve.tensor_scalar(dst, V[:, q, s - 1, 0:blocks], float(r + 1 - MARK), None, ALU.is_equal)
                if finish:
                    last.then_inc(s_hot, 1)

            def reduce_pair(i, q, s, p):
                dve.wait_ge(s_pair, pair_no(i, q, s, p) + 1)
                dve.tensor_reduce(part[:, par(q, s), BANK + p],
                                  pairs[buffer_of(s, p)][:, :, :, :].rearrange("f a k i -> f i (a k)"),
                                  AX.X, ALU.max).then_inc(s_used, 1)

            def extra_hots(q, s):
                for r in range(DEEPER):
                    for a, z in runs(DEPTHS[s]):
                        last = dve.tensor_scalar(hotx[:, r, a:z], V[:, q, s - 1, a:z],
                                                 float(DEPTHS[s][a] + r + 1 - MARK), None, ALU.is_equal)
                last.then_inc(s_hotx, 1)

            def extra_reduce(i, q, s):
                for p in range(EXTRA):
                    dve.wait_ge(s_xpair, EXTRA * pos(i, q, s) + p + 1)
                    dve.tensor_reduce(more[:, p], pairs[buffer_of(s, PAIRS[s] + p)][:, :, :, :]
                                      .rearrange("f a k i -> f i (a k)"), AX.X, ALU.max).then_inc(s_xused, 1)
                dve.drain()
                maxima = part[:, par(q, s), BANK:BANK + EXTRA]
                dve.tensor_tensor(maxima, maxima, more[:, :, :], ALU.max).then_inc(s_xdone, 1)

            def step_written(batch, st):
                if st > 0:
                    dve.wait_ge(s_ex, LAST_STEP * batch + st)

            def extraction(w, batch, steps, bp, drained=True):
                def after_last(st):
                    if drained:
                        dve.drain()

                for st in steps:
                    if st == 0:
                        ins = dve.scalar_tensor_tensor(out=g_score[w][:, :], in0=g_adj[w][:, :], scalar=0.0,
                                                       in1=falling[:, :], op0=ALU.not_equal, op1=ALU.mult)
                    elif st < LAST_STEP:
                        r = (st - 1) // 2
                        val = g_val[w][:, RANKS8 * r:RANKS8 * (r + 1)]
                        after_last(st)
                        if st % 2:
                            ins = dve.max(val, g_score[w][:, :])
                        else:
                            ins = dve.match_replace(g_score[w][:, :], val, g_score[w][:, :], 0.0)
                    else:
                        val, pick = g_val[w], g_pick[w]
                        after_last(st)
                        dve.scalar_tensor_tensor(out=pick[:, :], in0=val[:, 0:K], scalar=0.0,
                                                 in1=val[:, 0:1].to_broadcast([P, K]),
                                                 op0=ALU.is_equal, op1=ALU.mult)
                        dve.tensor_scalar(g_bound[w][:, bp, 0:1], val[:, K:K + 1], 0.0, -BIG, ALU.is_gt, ALU.mult)
                        dve.tensor_scalar(g_bound[w][:, bp, 1:2], val[:, 0:1], 0.0, None, ALU.is_gt)
                        dve.drain()
                        dve.scalar_tensor_tensor(out=pick[:, :], in0=pick[:, :], scalar=1.0, in1=val[:, 0:K],
                                                 op0=ALU.max, op1=ALU.max)
                        dve.drain()
                        dve.scalar_tensor_tensor(out=g_idx[w][:, :], in0=pick[:, :], scalar=-1.0,
                                                 in1=row_base[:, bass.ds(batch, 1)].to_broadcast([P, K]),
                                                 op0=ALU.mult, op1=ALU.add
                                                 ).then_inc(s_idx0 if w == 0 else s_fidx, 1)
                        continue
                    if w == 0:
                        ins.then_inc(s_ex, 1)

            def gathered_max(w, bp, signal):
                dve.tensor_reduce(g_max[w][:, :], g_feat[w][:, :, :].rearrange("p k f -> p f k"), AX.X,
                                  ALU.max).then_inc(s_g0max if w == 0 else s_fstep, 1)
                dve.drain()
                dve.tensor_scalar(g_agg[w][:, :], g_max[w][:, :], g_bound[w][:, bp, 0:1], g_bound[w][:, bp, 1:2],
                                  ALU.max, ALU.mult).then_inc(signal, 1)

            def redo(i, q, s):
                m = pos(i, q, s)
                dve.wait_ge(s_fadj, m + 1)
                extraction(1, 2 * i + q, range(LAST_STEP + 1), 0)
                dve.wait_ge(s_fg, m + 1)
                gathered_max(1, 0, s_fagg)
                dve.wait_ge(s_ft, m + 1)
                dve.wait_ge(s_halfc, m + 1)
                for p in range(BANK + PAIRS[s]):
                    last = dve.tensor_copy(part[:, par(q, s), p], p_xt)
                last.then_inc(s_xdone, 1)

            def merge(i, q, s):
                m = pos(i, q, s)
                dve.wait_ge(s_used, pair_no(i, q, s, PAIRS[s]))
                dve.wait_ge(s_xdone, m + 1)
                dve.wait_ge(s_halfc, m + 1)
                dve.tensor_reduce(agg_t[:, par(q, s)], part[:, par(q, s), 0:BANK + PAIRS[s]].rearrange("f k i -> f i k"), AX.X,
                                  ALU.max).then_inc(s_agg, 1)

            def count_violations(i, q):
                dve.wait_ge(s_cnt, MT * (2 * i + q + 1))
                if not is_first(i, q):
                    dve.wait_ge(s_relu, NT * (2 * i + q) - 1)
                cnt = p_cnt.rearrange("p (o t b) -> p o t b", o=1, b=NT)
                for lv in range(LEVELS):
                    dve.tensor_tensor(viol[:, lv, :, 0:NT], cnt[:, 0], depth_tab[:, lv], ALU.is_gt)
                dve.tensor_reduce(degree[:, :], cnt[:, 0], AX.X, ALU.add)
                dve.drain()
                for lv in range(LEVELS):
                    last = dve.tensor_scalar(viol[:, lv, :, NT], degree[:, :], float(K), None, ALU.is_gt)
                last.then_inc(s_viol, 1)

            def set_levels(i, q):
                dve.wait_ge(s_vp, 2 * i + q + 1)
                dve.tensor_reduce(vsum[:, :, :], p_viol.rearrange("p (l t b) -> p l t b", l=LEVELS, b=NT + 1),
                                  AX.X, ALU.add)
                dve.drain()
                dve.tensor_scalar(vsum[:, :, :], vsum[:, :, :], 1.0, None, ALU.min)
                dve.drain()
                dve.scalar_tensor_tensor(out=level[:, q], in0=vsum[:, 1], scalar=float(LEVELS), in1=vsum[:, 0],
                                         op0=ALU.mult, op1=ALU.max).then_inc(s_level, 1)

            def affine(q, count, a=0, z=NT):
                dve.wait_ge(s_std, count)
                dve.reciprocal(rstd[:, q, a:z], std[:, q, a:z])
                dve.drain()
                dve.tensor_tensor(shift[:, q, a:z], mean_neg[:, q, a:z], rstd[:, q, a:z], ALU.mult
                                  ).then_inc(s_affine, 1)

            EXTRACT = {1: {1: 0, 4: 1}, 2: {3: 2}, 3: {3: 3}, 4: {2: 4}, 5: {1: 5, 2: 6}, 6: {}, 7: {1: 7, 2: 8}}

            def step(i, q, last):
                ni, nq = following(i, q)
                pi, pq = preceding(i, q)
                begin = is_first(i, q)
                for s in range(1, NT):
                    m = pos(i, q, s)
                    nxt = (i, q, s + 1) if s < MT else None if last else (ni, nq, 1)
                    steps = {} if last else EXTRACT[s]
                    gaps = PAIRS[s] - 1
                    for p in range(PAIRS[s]):
                        if p in steps:
                            step_written(2 * i + q + 1, steps[p])
                        reduce_pair(i, q, s, p)
                        if p == 0:
                            if s > 1:
                                merge(i, q, s - 1)
                            elif not begin:
                                merge(pi, pq, MT)
                        if p == 0 and s == 1:
                            count_violations(i, q)
                        if p == 2 and s == 1:
                            set_levels(i, q)
                        if p == (1 if s > 1 else 3):
                            lv = load_level(i, q, s)
                        if p < gaps and nxt:
                            one_hots(*nxt, range(ACT_RANKS + p, DEPTHS[nxt[2]][0], gaps), p == gaps - 1)
                        if p in steps:
                            if steps[p] == 0:
                                dve.wait_ge(s_ex, LAST_STEP * (2 * i + q + 1))
                                dve.wait_ge(s_adj0, 16 * (2 * i + q + 2))
                            extraction(0, 2 * i + q + 1, (steps[p],), nq, False)
                        if p == 0 and s == 6 and not begin:
                            affine(pq, 2 * i + q)
                    with dve.If(lv > 0):
                        with dve.If(lv < LEVELS):
                            extra_hots(q, s)
                            extra_reduce(i, q, s)
                            dve.sem_inc(s_fidx, 1)
                            dve.sem_inc(s_fagg, 1)
                        with dve.Else():
                            redo(i, q, s)
                            dve.sem_inc(s_hotx, 1)
                            dve.sem_inc(s_xused, EXTRA)
                    with dve.Else():
                        dve.sem_inc(s_hotx, 1)
                        dve.sem_inc(s_xused, EXTRA)
                        dve.sem_inc(s_xdone, 1)
                        dve.sem_inc(s_fidx, 1)
                        dve.sem_inc(s_fagg, 1)
                    if s == 6:
                        dve.wait_ge(s_g0, 16 * K * (2 * i + q + 1))
                        gathered_max(0, q, s_agg0)

            def first_V(t):
                dve.wait_ge(s_Vp, 2 * t)
                dve.tensor_copy(V[:, 0, t - 1], pairs[t % 2][:, :, :, :].rearrange("p a k i -> p (a k) i")
                                ).then_inc(s_V, 2)

            def load_level(i, q, s):
                if s == 1:
                    dve.wait_ge(s_level, 2 * i + q + 1)
                    dve.nop(nofuse=True)
                return dve.value_load(level[0:1, q, s - 1:s], min_val=0, max_val=LEVELS)

            dve.wait_ge(s_falling, 1)
            dve.wait_ge(s_adj0, 16)
            for st in range(LAST_STEP + 1):
                if st == LAST_STEP:
                    dve.wait_ge(s_tab, TABLES)
                step_written(0, st)
                extraction(0, 0, (st,), 0, False)
                t = st - (LAST_STEP - MT + 1)
                if t >= 1:
                    first_V(t)
            one_hots(0, 0, 1, range(ACT_RANKS, DEPTHS[1][0]), True)
            first_V(MT)
            run(dve, step)
            merge(B // 2 - 1, 1, MT)
            for part_no, (a, z) in enumerate(((0, MT), (MT, NT))):
                affine(1, B + part_no, a, z)
                dve.drain()
                for t in range(a, z):
                    dve.tensor_scalar(y_sb[:, 1, t], y_sb[:, 1, t], rstd[:, 1, t:t + 1], shift[:, 1, t:t + 1],
                                      ALU.mult, ALU.add).then_inc(s_norm, 1)

        @block.tensor
        def _(pe):
            def transpose_mask(i, q, s):
                n = pos(i, q, s)
                pe.wait_ge(s_mask, n + 1)
                if not (isinstance(n, int) and n < 1):
                    pe.wait_ge(s_mTc, n)
                for kb in range(NT):
                    last = pe.transpose(p_maskT[:, kb * P:(kb + 1) * P], mask[:, par(q, s), kb * P:(kb + 1) * P],
                                        ident_bf[:, :])
                last.then_inc(s_mT, 1)

            def rank_product(i, q, s, h, m):
                n = pos(i, q, s)
                if h == 0:
                    pe.wait_ge(s_mTc, n + 1)
                if not (isinstance(n, int) and 2 * n + h < 1):
                    pe.wait_ge(s_V, 2 * n + h)
                pe.wait_ge(s_xtc, m + 1)
                pe.matmul(p_V[:, :], rank_bf[:, :], maskT[:, par(q, s), h * N // 2:(h + 1) * N // 2],
                          start=True, stop=True).then_inc(s_Vp, 1)

            def count(i, q, s):
                n = pos(i, q, s)
                if s == 1 and not (isinstance(n, int) and n < 1):
                    pe.wait_ge(s_viol, 2 * i + q)
                pe.wait_ge(s_mTc, n + 1)
                for kb in range(NT):
                    c = (s - 1) * NT + kb
                    last = pe.matmul(p_cnt[:, c:c + 1], maskT[:, par(q, s), kb * P:(kb + 1) * P], ones_bf[:, :],
                                     start=True, stop=True)
                last.then_inc(s_cnt, 1)

            def pick(dst, q, kb, one_hot, signal=None):
                for part_no in range(3):
                    last = pe.matmul(dst, x_part[:, q, part_no, kb], one_hot, start=(part_no == 0),
                                     stop=(part_no == 2))
                if signal is not None:
                    last.then_inc(signal, 1)

            def pick_bank(dst, q, s, bank, signal=None):
                u = par(q, s)
                for kb, r, n, place in bank:
                    one_hot = hot[:, u, r:r + n, kb] if r < LOW else hot_high[:, u, r - LOW:r - LOW + n, kb]
                    pick(dst[:, place:place + n], q, kb, one_hot, signal if place + n == BANK else None)

            def pick_pair(i, q, s, p):
                m = pos(i, q, s)
                start = isinstance(m, int) and m == 0
                if p == 0:
                    pe.wait_ge(s_hot, m + 1)
                    pe.wait_ge(s_hot2, m + 1)
                    if not start:
                        pe.wait_ge(s_xused, EXTRA * m)
                if start and p < 2:
                    pe.wait_ge(s_V, 2 * (MT - 1 + p))
                else:
                    pe.wait_ge(s_used, pair_no(i, q, s, p) - 1)
                dst = pairs[buffer_of(s, p)]
                pick_bank(dst[:, 0], q, s, BANKS[s][2 * p])
                pick_bank(dst[:, 1], q, s, BANKS[s][2 * p + 1], s_pair)

            def pick_half(i, q, s):
                m = pos(i, q, s)
                if not (isinstance(m, int) and m == 0):
                    pe.wait_ge(s_halfc, m)
                pick_bank(half, q, s, BANKS[s][2 * PAIRS[s]], s_half)

            def extra_level(i, q, s):
                pe.wait_ge(s_hotx, pos(i, q, s) + 1)
                each = NT // EXTRA
                for p in range(EXTRA):
                    pe.wait_ge(s_used, pair_no(i, q, s, PAIRS[s] + p) - 1)
                    dst = pairs[buffer_of(s, PAIRS[s] + p)].rearrange("f a (k r) i -> f (a k) r i", r=DEEPER)
                    for j in range(each):
                        kb = each * p + j
                        pick(dst[:, j], q, kb, hotx[:, :, kb], s_xpair if j == each - 1 else None)

            def turn_features(q, t, signal):
                for part_no in range(3):
                    last = pe.matmul(p_xt, x_part[:, q, part_no, t], ident_bf[:, :], start=(part_no == 0),
                                     stop=(part_no == 2))
                last.then_inc(signal, 1)

            def transpose_x(i, q, s, vcopies):
                m = pos(i, q, s)
                if not (isinstance(m, int) and m == 0):
                    pe.wait_ge(s_xtc, m)
                pe.wait_ge(s_V, vcopies)
                turn_features(q, s, s_xt)

            def linear(xt, agg, signal):
                pe.matmul(p_out, xt, w_sb[:, 0], start=True, stop=False)
                pe.matmul(p_out, agg, w_sb[:, 1], start=False, stop=False)
                pe.matmul(p_out, ones_row[:, :], bias[:, :], start=False, stop=True).then_inc(signal, 1)

            def out_free(i, q, order):
                if not (isinstance(i, int) and i == 0 and q == 0 and order <= 0):
                    pe.wait_ge(s_relu, NT * (2 * i + q) + order)

            def linear_main(i, q, s):
                m = pos(i, q, s)
                out_free(i, q, ORDER[s])
                pe.wait_ge(s_xtc, m + 1)
                pe.wait_ge(s_agg, m + 1)
                linear(xt_sb[:, par(q, s)], agg_t[:, par(q, s)], s_out)

            def violations(i, q):
                pe.wait_ge(s_viol, 2 * i + q + 1)
                pe.matmul(p_viol, ones_bf[:, :], viol[:, :, :, :].rearrange("p l t b -> p (l t b)"), start=True, stop=True).then_inc(s_vp, 1)

            def step(i, q, last):
                ni, nq = following(i, q)
                pi, pq = preceding(i, q)
                begin = is_first(i, q)
                for s in range(1, NT):
                    m = pos(i, q, s)
                    if s == 1:
                        pe.wait_ge(s_split, 2 * i + q + 1)
                    vc = 2 * pos(ni, nq, s) if not last else 2 * MAIN
                    pick_pair(i, q, s, 0)
                    if s == 5:
                        pe.wait_ge(s_xtc, m)
                        pe.wait_ge(s_V, vc)
                        turn_features(q, 0, s_x0t)
                    if not last:
                        transpose_mask(ni, nq, s)
                    pick_pair(i, q, s, 1)
                    if s == 5:
                        pe.wait_ge(s_x0c, 2 * i + q + 1)
                    transpose_x(i, q, s, vc)
                    if s > 1:
                        out_free(i, q, ORDER[s - 1])
                        if not last:
                            count(ni, nq, s)
                    pick_pair(i, q, s, 2)
                    if s == MT:
                        pe.wait_ge(s_xtc, m + 1)
                        pe.wait_ge(s_V, vc)
                        pe.wait_ge(s_agg0, 2 * i + q + 1)
                        pe.transpose(p_xt, g_agg[0][:, :], ident[:, :]).then_inc(s_agg0t, 1)
                    if s > 1:
                        linear_main(i, q, s - 1)
                    if s == 1:
                        violations(i, q)
                    if s == MT:
                        pe.wait_ge(s_agg0c, 2 * i + q + 1)
                    if not last:
                        rank_product(ni, nq, s, 0, m)
                    pick_pair(i, q, s, 3)
                    if s == 1:
                        pick_pair(i, q, s, 4)
                        pe.wait_ge(s_level, 2 * i + q + 1)
                        if not begin:
                            out_free(i, q, -1)
                        if not last:
                            count(ni, nq, s)
                        if not begin:
                            linear_main(pi, pq, MT)
                        pe.nop(nofuse=True)
                    lv = pe.value_load(level[0:1, q, s - 1:s], min_val=0, max_val=LEVELS)
                    for p in range(5 if s == 1 else 4, PAIRS[s]):
                        pick_pair(i, q, s, p)
                    pick_half(i, q, s)
                    if s == MT:
                        out_free(i, q, ORDER[0])
                        linear(x0_t[:, :], agg0_t[:, :], s_out0)
                    with pe.If(lv > 0):
                        with pe.If(lv < LEVELS):
                            extra_level(i, q, s)
                            pe.sem_inc(s_ft, 1)
                        with pe.Else():
                            pe.sem_inc(s_xpair, EXTRA)
                            pe.wait_ge(s_fagg, m + 1)
                            pe.wait_ge(s_xtc, m + 1)
                            pe.wait_ge(s_V, vc + 1 if not last else vc)
                            pe.transpose(p_xt, g_agg[1][:, :], ident[:, :]).then_inc(s_ft, 1)
                            pe.wait_ge(s_xdone, m + 1)
                    with pe.Else():
                        pe.sem_inc(s_xpair, EXTRA)
                        pe.sem_inc(s_ft, 1)
                    if not last:
                        rank_product(ni, nq, s, 1, m)

            pe.wait_ge(s_tab, TABLES)
            pe.wait_ge(s_tab2, 2)
            transpose_mask(0, 0, 1)
            for s in range(1, NT):
                if s < MT:
                    transpose_mask(0, 0, s + 1)
                pe.wait_ge(s_mTc, s)
                if s > 2:
                    pe.wait_ge(s_V, 2 * (s - 2))
                for h in range(2):
                    pe.matmul(pairs[s % 2][:, h], rank_bf[:, :], maskT[:, par(0, s), h * N // 2:(h + 1) * N // 2],
                              start=True, stop=True).then_inc(s_Vp, 1)
                count(0, 0, s)
            pe.wait_ge(s_const, 32)
            run(pe, step)
            linear_main(B // 2 - 1, 1, MT)


def kernel(x, adj, L0_gnn_W, L0_gnn_b):
    import numpy as np
    import concourse.bacc as bacc
    from concourse.bass_utils import run_bass_kernel_spmd as run

    nc = bacc.Bacc("TRN2", target_bir_lowering=False, num_devices=1)
    arrays, args = {}, []
    for name, a in (("x", x), ("adj", adj), ("W", L0_gnn_W), ("b", L0_gnn_b)):
        a = np.ascontiguousarray(a)
        arrays["in_" + name] = a
        args.append(nc.dram_tensor("in_" + name, a.shape, mybir.dt.from_np(a.dtype), kind="ExternalInput").ap())
    out = nc.dram_tensor("out", x.shape, F32, kind="ExternalOutput").ap()
    build(nc, *args, out)
    r = run(nc, [arrays], core_ids=[0])
    return r.results[0]["out"]
```
